# Optimizing a Trainium2 kernel written in Bass

```python
import numpy as np
import jax
import jax.numpy as jnp

def _softmax(x, axis=-1):
    return jax.nn.softmax(x, axis=axis)
def _gelu(x):
    return jax.nn.gelu(x, approximate=True)
def _silu(x):
    return jax.nn.silu(x)
def _sigmoid(x):
    return jax.nn.sigmoid(x)
def _layernorm(x, axis=-1, eps=1e-5):
    m = jnp.mean(x, axis=axis, keepdims=True)
    v = jnp.var(x, axis=axis, keepdims=True)
    return (x - m) / jnp.sqrt(v + eps)
def _scatter_add(tgt, idx, src, axis=0):
    return tgt.at[idx].add(src)
def _segment_sum(src, seg, n):
    return jax.ops.segment_sum(src, seg, n)

kernel_name = 'mk_conv_preact_d2_conv_nchw96_cb91d3'

def setup_inputs(seed: int = 0):
    np.random.seed(seed)
    _w = jnp.asarray
    def _rec_inputs():
        import jax
        import jax.numpy as jnp
        _gk = jax.random.key(seed)
        x = -4.65e-05 + 0.9999 * jax.random.normal(jax.random.fold_in(_gk, 1), (8, 96, 256, 256), jnp.float32)
        return x
    x = _rec_inputs()
    def _L0_conv_setup():
        import jax, jax.numpy as jnp
        import numpy as np
        WS = 16
        NH = 8
        EPS = 1e-06
        BN_EPS = 1e-05

        def _l2norm(t):
            return t / jnp.linalg.norm(t, axis=-2, keepdims=True)
        key = jax.random.key(seed)
        k1, k2, k3 = jax.random.split(key, 3)
        B, C, H, W = (8, 96, 256, 256)
        x = jax.random.normal(k1, (B, C, H, W), dtype=jnp.float32)
        w_qkv = jax.random.normal(k2, (3 * C, C), dtype=jnp.float32) * (1.0 / np.sqrt(C))
        w_proj = jax.random.normal(k3, (C, C), dtype=jnp.float32) * (1.0 / np.sqrt(C))
        gamma = jnp.ones((C,), dtype=jnp.float32)
        beta = jnp.zeros((C,), dtype=jnp.float32)
        return {'x': x, 'w_qkv': w_qkv, 'w_proj': w_proj, 'gamma': gamma, 'beta': beta}
    _L0_conv_all = _L0_conv_setup()
    _L0_conv_in = {k: v for k, v in _L0_conv_all.items() if k in ('w_qkv', 'w_proj', 'gamma', 'beta', )}
    del _L0_conv_all

    def _L1_conv_setup():
        import jax, jax.numpy as jnp
        import numpy as np
        WT_LEVELS = 3

        def haar2d(x):
            a = x[:, :, 0::2, 0::2]
            b = x[:, :, 0::2, 1::2]
            c = x[:, :, 1::2, 0::2]
            d = x[:, :, 1::2, 1::2]
            ll = (a + b + c + d) * 0.5
            lh = (a - b + c - d) * 0.5
            hl = (a + b - c - d) * 0.5
            hh = (a - b - c + d) * 0.5
            return jnp.stack([ll, lh, hl, hh], axis=2)

        def ihaar2d(co):
            ll, lh, hl, hh = (co[:, :, 0], co[:, :, 1], co[:, :, 2], co[:, :, 3])
            a = (ll + lh + hl + hh) * 0.5
            b = (ll - lh + hl - hh) * 0.5
            c = (ll + lh - hl - hh) * 0.5
            d = (ll - lh - hl + hh) * 0.5
            B, C, h, w = ll.shape
            top = jnp.stack([a, b], axis=-1).reshape(B, C, h, 2 * w)
            bot = jnp.stack([c, d], axis=-1).reshape(B, C, h, 2 * w)
            return jnp.stack([top, bot], axis=3).reshape(B, C, 2 * h, 2 * w)

        def dwconv(x, w):
            return jax.lax.conv_general_dilated(x, w, (1, 1), 'SAME', dimension_numbers=('NCHW', 'OIHW', 'NCHW'), feature_group_count=x.shape[1])
        key = jax.random.key(seed)
        ks = jax.random.split(key, 5)
        B, C, H, W, K, L = (8, 96, 224, 224, 5, WT_LEVELS)
        x = jax.random.normal(ks[0], (B, C, H, W), jnp.float32)
        base_w = jax.random.normal(ks[1], (C, 1, K, K), jnp.float32) * 0.1
        base_b = jax.random.normal(ks[2], (C,), jnp.float32) * 0.01
        base_scale = jnp.ones((1, C, 1, 1), jnp.float32)
        wconv_w = jax.random.normal(ks[3], (L, 4 * C, 1, K, K), jnp.float32) * 0.1
        wscale = jnp.full((L, 1, 4 * C, 1, 1), 0.1, jnp.float32)
        return {'x': x, 'base_w': base_w, 'base_b': base_b, 'base_scale': base_scale, 'wconv_w': wconv_w, 'wscale': wscale}
    _L1_conv_all = _L1_conv_setup()
    _L1_conv_in = {k: v for k, v in _L1_conv_all.items() if k in ('base_w', 'base_b', 'base_scale', 'wconv_w', 'wscale', )}
    del _L1_conv_all

    return {
        "x": x,
        "L0_conv_w_qkv": _L0_conv_in["w_qkv"],
        "L0_conv_w_proj": _L0_conv_in["w_proj"],
        "L0_conv_gamma": _L0_conv_in["gamma"],
        "L0_conv_beta": _L0_conv_in["beta"],
        "L1_conv_base_w": _L1_conv_in["base_w"],
        "L1_conv_base_b": _L1_conv_in["base_b"],
        "L1_conv_base_scale": _L1_conv_in["base_scale"],
        "L1_conv_wconv_w": _L1_conv_in["wconv_w"],
        "L1_conv_wscale": _L1_conv_in["wscale"],
    }

def reference(x, L0_conv_w_qkv, L0_conv_w_proj, L0_conv_gamma, L0_conv_beta, L1_conv_base_w, L1_conv_base_b, L1_conv_base_scale, L1_conv_wconv_w, L1_conv_wscale):
    import jax
    import jax.numpy as jnp
    def _L0_conv_ref(x, w_qkv, w_proj, gamma, beta):
        import jax, jax.numpy as jnp
        import numpy as np
        WS = 16
        NH = 8
        EPS = 1e-06
        BN_EPS = 1e-05

        def _l2norm(t):
            return t / jnp.linalg.norm(t, axis=-2, keepdims=True)
        B, C, H, W = x.shape
        ws, nh = (WS, NH)
        d = C // nh
        Hp = (H + ws - 1) // ws * ws
        Wp = (W + ws - 1) // ws * ws
        if (Hp, Wp) != (H, W):
            x = jnp.pad(x, ((0, 0), (0, 0), (0, Hp - H), (0, Wp - W)))
        hh, ww = (Hp // ws, Wp // ws)
        qkv = jnp.einsum('oc,bchw->bohw', w_qkv, x)
        qkv = qkv.reshape(B, 3, nh, d, hh, ws, ww, ws)
        qkv = qkv.transpose(1, 0, 4, 6, 2, 3, 5, 7).reshape(3, B * hh * ww, nh, d, ws * ws)
        q, k, v = (qkv[0], qkv[1], qkv[2])
        q = _l2norm(q).transpose(0, 1, 3, 2)
        k = _l2norm(k)
        ksum = k.sum(axis=-1) + EPS
        tailor = 1.0 / (ws * ws + jnp.einsum('bhnc,bhc->bhn', q, ksum))
        kv = jnp.einsum('bhmn,bhcn->bhmc', k, v)
        attn = jnp.einsum('bhnm,bhmc->bhcn', q, kv)
        attn = attn + v.sum(axis=-1, keepdims=True)
        attn = attn * tailor[:, :, None, :]
        out = attn.reshape(B, hh, ww, nh, d, ws, ws)
        out = out.transpose(0, 3, 4, 1, 5, 2, 6).reshape(B, C, Hp, Wp)
        out = out[:, :, :H, :W]
        y = jnp.einsum('oc,bchw->bohw', w_proj, out)
        mean = y.mean(axis=(0, 2, 3), keepdims=True)
        var = y.var(axis=(0, 2, 3), keepdims=True)
        y = (y - mean) * jax.lax.rsqrt(var + BN_EPS)
        y = y * gamma[None, :, None, None] + beta[None, :, None, None]
        return y

    def _L1_conv_ref(x, base_w, base_b, base_scale, wconv_w, wscale):
        import jax, jax.numpy as jnp
        import numpy as np
        WT_LEVELS = 3

        def haar2d(x):
            a = x[:, :, 0::2, 0::2]
            b = x[:, :, 0::2, 1::2]
            c = x[:, :, 1::2, 0::2]
            d = x[:, :, 1::2, 1::2]
            ll = (a + b + c + d) * 0.5
            lh = (a - b + c - d) * 0.5
            hl = (a + b - c - d) * 0.5
            hh = (a - b - c + d) * 0.5
            return jnp.stack([ll, lh, hl, hh], axis=2)

        def ihaar2d(co):
            ll, lh, hl, hh = (co[:, :, 0], co[:, :, 1], co[:, :, 2], co[:, :, 3])
            a = (ll + lh + hl + hh) * 0.5
            b = (ll - lh + hl - hh) * 0.5
            c = (ll + lh - hl - hh) * 0.5
            d = (ll - lh - hl + hh) * 0.5
            B, C, h, w = ll.shape
            top = jnp.stack([a, b], axis=-1).reshape(B, C, h, 2 * w)
            bot = jnp.stack([c, d], axis=-1).reshape(B, C, h, 2 * w)
            return jnp.stack([top, bot], axis=3).reshape(B, C, 2 * h, 2 * w)

        def dwconv(x, w):
            return jax.lax.conv_general_dilated(x, w, (1, 1), 'SAME', dimension_numbers=('NCHW', 'OIHW', 'NCHW'), feature_group_count=x.shape[1])
        B, C, H, W = x.shape
        cur = x
        level_coeffs = []
        for i in range(WT_LEVELS):
            co = haar2d(cur)
            cur = co[:, :, 0]
            h, w = co.shape[-2:]
            flat = co.reshape(B, C * 4, h, w)
            flat = dwconv(flat, wconv_w[i]) * wscale[i]
            level_coeffs.append(flat.reshape(B, C, 4, h, w))
        next_ll = jnp.zeros_like(level_coeffs[-1][:, :, 0])
        for i in reversed(range(WT_LEVELS)):
            co = level_coeffs[i].at[:, :, 0].add(next_ll)
            next_ll = ihaar2d(co)
        base = dwconv(x, base_w) * base_scale + base_b.reshape(1, C, 1, 1)
        return base + next_ll

    def _gn(v, G=32, eps=1e-5):
        B_, C_, H_, W_ = v.shape
        g = v.reshape(B_, G, C_ // G, H_, W_)
        m = jnp.mean(g, axis=(2, 3, 4), keepdims=True)
        s = jnp.var(g, axis=(2, 3, 4), keepdims=True)
        return ((g - m) / jnp.sqrt(s + eps)).reshape(v.shape)

    def _ln_c(v, eps=1e-6):
        m = jnp.mean(v, axis=1, keepdims=True)
        s = jnp.var(v, axis=1, keepdims=True)
        return (v - m) / jnp.sqrt(s + eps)

    def _ln_t(v, eps=1e-5):
        m = jnp.mean(v, axis=-1, keepdims=True)
        s = jnp.var(v, axis=-1, keepdims=True)
        return (v - m) / jnp.sqrt(s + eps)

    def _to_tokens(v):
        B_, C_, H_, W_ = v.shape
        return v.reshape(B_, C_, H_ * W_).transpose(0, 2, 1)
    def _from_tokens(t, like):
        B_, C_, H_, W_ = like.shape
        return t.transpose(0, 2, 1).reshape(B_, C_, H_, W_)

    x = x + _L0_conv_ref(_gn(x), L0_conv_w_qkv, L0_conv_w_proj, L0_conv_gamma, L0_conv_beta)
    x = x + _L1_conv_ref(_gn(x), L1_conv_base_w, L1_conv_base_b, L1_conv_base_scale, L1_conv_wconv_w, L1_conv_wscale)
    return x


_drawn_inputs = setup_inputs


def setup_inputs(seed=0):
    import zlib

    import numpy as np

    out = dict(_drawn_inputs(seed))
    spreads = {'L0_conv_gamma': (1.0, 0.2),
     'L0_conv_beta': (0.0, 0.1),
     'L1_conv_base_scale': (1.0, 0.2),
     'L1_conv_wscale': (0.10000000149011612, 0.6)}
    factors = {'L1_conv_base_b': 8.0}
    for name, (base, spread) in spreads.items():
        noise = np.random.default_rng([zlib.crc32(name.encode()), seed]).standard_normal(out[name].shape)
        drawn = base * np.exp(spread * noise) if base else spread * noise
        out[name] = jnp.asarray(drawn.astype(out[name].dtype))
    for name, factor in factors.items():
        out[name] = (out[name] * factor).astype(out[name].dtype)
    return out
```

```python
from contextlib import ExitStack

import concourse.bass as bass
from concourse import mybir

F32 = mybir.dt.float32
ALU = mybir.AluOpType
ACT = mybir.ActivationFunctionType
AX = mybir.AxisListType

B, C, H, W = 8, 96, 256, 256
WS, NH = 16, 8
HD = C // NH
GROUPS = 32
ROWS_STRIP = WS
STRIPS_IMG = H // ROWS_STRIP
STRIPS = B * STRIPS_IMG
STRIP = ROWS_STRIP * W
PAIRS = W // WS // 2
WIN = WS * WS
TOK = 2 * WIN
TG = TOK // 128
LAST = STRIPS * PAIRS
STAT = 6
GN_EPS, BN_EPS, K_EPS = 1e-5, 1e-5, 1e-6

TAPS = 5
HALF = W // 2
WROWS = 64
HALO = 4
OROWS = 52
WINDOWS = -(-H // OROWS)
PAIRW = -(-WINDOWS // 2)
IMGS = 4
SETS = B // IMGS
ZW = HALF + 4
V1 = 2 * WROWS
V2 = 2 * HALF
NV1 = 4 * TAPS * 2
NV2 = 2 * 2 * TAPS
NPAR = 2 + 2 * B


def window_rows(t):
    start = OROWS * t - HALO
    lo, hi = max(0, start), min(H, start + WROWS)
    return lo, hi, lo - start


def wt_attention_kernel(nc, x, wq_t, wkv_t, wp_t, gamma, beta, base_w, base_b, base_scale, wconv, wscale,
                        ident, gmean, head96, head8, keps, down, up, inside, out):
    y_dram = nc.dram_tensor("y_scratch", [B, C, H, W], F32, kind="Internal").ap()
    vec1 = nc.dram_tensor("vec1", [C, NV1 * V1], F32, kind="Internal").ap()
    vec2 = nc.dram_tensor("vec2", [C, NV2 * V2], F32, kind="Internal").ap()
    vec3 = nc.dram_tensor("vec3", [C, NV2 * V2], F32, kind="Internal").ap()
    par_dram = nc.dram_tensor("params", [C, NPAR], F32, kind="Internal").ap()
    x_strips = x.rearrange("b c (s r) w -> b s c (r w)", r=ROWS_STRIP)
    y_strips = y_dram.rearrange("b c (s r) w -> b s c (r w)", r=ROWS_STRIP)

    with ExitStack() as ctx:
        def sb(name, shape):
            return ctx.enter_context(nc.sbuf_tensor(name, shape, F32))

        def sem(name):
            return ctx.enter_context(nc.semaphore(name))

        XY = 2 * STRIP
        arena = sb("arena", [128, 31232])
        xs = arena[0:C, 0:XY].rearrange("p (k n) -> p k n", k=2)
        stat_x = arena[0:C, XY:XY + B * 128 * STAT].rearrange("p (b n) -> p b n", b=B)
        at = XY + B * 128 * STAT
        ys = arena[0:C, at:at + XY].rearrange("p (k n) -> p k n", k=2)
        stat_y = arena[0:C, at + XY:at + XY + LAST * STAT]
        pad1 = arena[0:C, at:at + NV1 * V1]
        pad2 = arena[0:C, at + NV1 * V1:at + NV1 * V1 + NV2 * V2]
        pad3 = arena[0:C, at + NV1 * V1 + NV2 * V2:at + NV1 * V1 + 2 * NV2 * V2]
        pads = arena[0:C, at:at + NV1 * V1 + 2 * NV2 * V2]
        assert at + XY + LAST * STAT <= 31232 and at + NV1 * V1 + 2 * NV2 * V2 <= 31232

        ident_sb = sb("ident_sb", [128, 128])
        gmean_sb = sb("gmean_sb", [C, C])
        mean_x = sb("mean_x", [C, B])
        var_x = sb("var_x", [C, B])
        gm0 = sb("gm0", [C, B])
        r0 = sb("r0", [C, B])
        nb0 = sb("nb0", [C, B])
        cxy_strip = sb("cxy_strip", [C, STRIPS])
        gb = sb("gb", [C, 4])

        with ExitStack() as ph:
            def ps_(name, shape):
                return ph.enter_context(nc.psum_tensor(name, shape, F32))

            def sem_(name):
                return ph.enter_context(nc.semaphore(name))

            def sb_(name, shape):
                return ph.enter_context(nc.sbuf_tensor(name, shape, F32))

            taps_b = sb_("taps_b", [C, TAPS * TAPS])
            taps_w = sb_("taps_w", [C, 3, 4, TAPS * TAPS])
            scale_w = sb_("scale_w", [C, 3, 4])
            scale_q = sb_("scale_q", [C, 3, 4])
            taps_s = sb_("taps_s", [C, 3, 4, TAPS * TAPS])
            sum_t = sb_("sum_t", [C, 3, 2, 2, TAPS * TAPS])
            full1 = sb_("full1", [C, 2, 2, TAPS, TAPS])
            base_t = sb_("base_t", [C, TAPS, TAPS])
            mv = sb_("mv", [C, B, 2])
            dev = sb_("dev", [C, B])
            tot = sb_("tot", [C, B])
            ps_m = ps_("ps_m", [C, 512])
            ps_v = ps_("ps_v", [C, 512])
            const_in = sem_("const_in")
            taps_in = sem_("taps_in")
            x_in = [sem_(f"x_in{k}") for k in range(2)]
            x_used = [sem_(f"x_used{k}") for k in range(2)]
            padded = sem_("padded")
            vec_out = sem_("vec_out")
            means = sem_("means")
            gmeans = sem_("gmeans")
            vars_ = sem_("vars")
            gvars = sem_("gvars")
            veps = sem_("veps")
            sd = sem_("sd")
            chain_p = sem_("chain_p")
            chain_v = sem_("chain_v")
            block = ph.enter_context(nc.Block())

            @block.sync
            def _(sp):
                with sp.Fori(0, B) as b:
                    with sp.Fori(0, STRIPS_IMG // 2) as h:
                        for k in range(2):
                            sp.wait_ge(x_used[k], b * (STRIPS_IMG // 2) + h + 1)
                            sp.dma_start(xs[:, k, :], x_strips[bass.ds(b, 1), bass.ds(h * 2 + k, 1)].squeeze()
                                         ).then_inc(x_in[k], 16)

            @block.scalar
            def _(act):
                act.dma_start(taps_b[:], base_w).then_inc(taps_in, 16)
                act.dma_start(taps_w[:], wconv).then_inc(taps_in, 16)
                act.dma_start(scale_w[:], wscale).then_inc(taps_in, 16)
                for i, v in enumerate((gamma, beta, base_b, base_scale)):
                    act.dma_start(gb[:, i:i + 1], v).then_inc(taps_in, 16)
                act.dma_start(ident_sb[:], ident).then_inc(const_in, 16)
                act.dma_start(gmean_sb[:], gmean).then_inc(const_in, 16)
                act.wait_ge(padded, 1)
                act.dma_start(vec1, pad1).then_inc(vec_out, 16)
                act.dma_start(vec2, pad2).then_inc(vec_out, 16)
                act.dma_start(vec3, pad3).then_inc(vec_out, 16)
                act.wait_ge(veps, 1)
                nc.scalar.activation(dev[:], tot[:], ACT.Sqrt).then_inc(sd, 1)
                act.wait_ge(vec_out, 48)

            @block.gpsimd
            def _(pool):
                steps = [0]

                def link(ins):
                    steps[0] += 1
                    ins.then_inc(chain_p, 1)
                    pool.wait_ge(chain_p, steps[0])

                g = nc.gpsimd
                link(g.memset(pads, 0.0))
                pool.wait_ge(taps_in, 16 * 7)
                for lv, f in ((0, 0.25), (1, 0.25), (2, 0.0625)):
                    link(g.tensor_scalar(scale_q[:, lv, :], scale_w[:, lv, :], f, None, ALU.mult))
                for lv in range(3):
                    for s in range(4):
                        link(g.tensor_scalar(taps_s[:, lv, s, :], taps_w[:, lv, s, :], scale_q[:, lv, s:s + 1], None,
                                             ALU.mult))
                for lv in range(3):
                    for ab in range(2):
                        for u in range(2):
                            link(g.tensor_tensor(sum_t[:, lv, ab, u, :], taps_s[:, lv, ab, :], taps_s[:, lv, ab + 2, :],
                                                 ALU.subtract if u else ALU.add))
                for u in range(2):
                    for v in range(2):
                        link(g.tensor_tensor(full1[:, u, v].rearrange("p a b -> p (a b)"), sum_t[:, 0, 0, u, :],
                                             sum_t[:, 0, 1, u, :], ALU.subtract if v else ALU.add))
                link(g.tensor_scalar(base_t[:].rearrange("p a b -> p (a b)"), taps_b[:], gb[:, 3:4], None, ALU.mult))
                p1 = pad1.rearrange("p (ia q dj o n) -> p ia q dj o n", ia=2, q=2, dj=TAPS, o=2)
                for ia in range(2):
                    for q in range(2):
                        for oa in range(2):
                            for p in range(2):
                                o = 1 - p
                                first = WROWS - 3 - oa
                                full = p1[:, ia, q, :, o, first:first + 2 * TAPS - 1:2]
                                link(g.tensor_copy(full, full1[:, (ia + oa) % 2, (q + p) % 2].rearrange("p di dj -> p dj di")))
                                dis = [k for k in range(TAPS) if 0 <= 2 * k + ia - oa - 2 < TAPS]
                                djs = [k for k in range(TAPS) if 0 <= 2 * k + q - p - 2 < TAPS]
                                r_, c_ = 2 * dis[0] + ia - oa - 2, 2 * djs[0] + q - p - 2
                                for n, dj in enumerate(djs):
                                    lo = first + 2 * dis[0]
                                    part = p1[:, ia, q, dj, o, lo:lo + 2 * len(dis) - 1:2]
                                    link(g.tensor_tensor(part, part, base_t[:, r_:r_ + 2 * len(dis) - 1:2, c_ + 2 * n],
                                                         ALU.add))
                p2 = pad2.rearrange("p (ia ab dj n) -> p ia ab dj n", ia=2, ab=2, dj=TAPS)
                p3 = pad3.rearrange("p (ia ab dj n) -> p ia ab dj n", ia=2, ab=2, dj=TAPS)
                for ia in range(2):
                    for ab in range(2):
                        for oa in range(2):
                            t2 = sum_t[:, 1, ab, (ia + oa) % 2, :].rearrange("p (di dj) -> p dj di", dj=TAPS)
                            first = HALF - 3 - oa
                            link(g.tensor_copy(p2[:, ia, ab, :, first:first + 2 * TAPS - 1:2], t2))
                        for rho in range(4):
                            t3 = sum_t[:, 2, ab, (ia + rho // 2) % 2, :].rearrange("p (di dj) -> p dj di", dj=TAPS)
                            first = HALF - 5 - rho
                            link(g.tensor_copy(p3[:, ia, ab, :, first:first + 4 * TAPS - 3:4], t3))
                pool.sem_inc(padded, 1)

            @block.tensor
            def _(pe):
                pe.wait_ge(const_in, 32)
                pe.wait_ge(means, 1)
                nc.tensor.matmul(ps_m[:, 0:B], gmean_sb[:], mean_x[:], start=True, stop=True).then_inc(gmeans, 1)
                pe.wait_ge(vars_, 1)
                nc.tensor.matmul(ps_v[:, 0:B], gmean_sb[:], tot[:], start=True, stop=True).then_inc(gvars, 1)

            @block.vector
            def _(dve):
                steps = [0]

                def link(ins):
                    steps[0] += 1
                    ins.then_inc(chain_v, 1)
                    dve.wait_ge(chain_v, steps[0])

                v = nc.vector
                for k in range(2):
                    dve.sem_inc(x_used[k], 1)
                stat_x_all = stat_x.rearrange("p b n -> p (b n)")
                with dve.Fori(0, B * STRIPS_IMG // 2) as h:
                    for k in range(2):
                        dve.wait_ge(x_in[k], (h + 1) * 16)
                        for j in range(STRIP // 512):
                            last = v.bn_stats(stat_x_all[:, bass.ds((h * 16 + (k * 8 + j)) * STAT, STAT)],
                                              xs[:, k, j * 512:(j + 1) * 512])
                        last.then_inc(x_used[k], 1)
                for k in range(2):
                    dve.wait_ge(x_used[k], STRIPS // 2 + 1)
                for b in range(B):
                    last = v.bn_aggr(mv[:, b, :], stat_x[:, b, :])
                link(last)
                v.tensor_copy(var_x[:], mv[:, :, 1])
                link(v.tensor_copy(mean_x[:], mv[:, :, 0]))
                dve.sem_inc(means, 1)
                dve.wait_ge(gmeans, 1)
                link(v.tensor_copy(gm0[:], ps_m[:, 0:B]))
                link(v.tensor_tensor(dev[:], mean_x[:], gm0[:], ALU.subtract))
                link(v.tensor_tensor(dev[:], dev[:], dev[:], ALU.mult))
                link(v.tensor_tensor(tot[:], dev[:], var_x[:], ALU.add))
                dve.sem_inc(vars_, 1)
                dve.wait_ge(gvars, 1)
                v.tensor_scalar(tot[:], ps_v[:, 0:B], GN_EPS, None, ALU.add).then_inc(veps, 1)
                dve.wait_ge(sd, 1)
                link(v.reciprocal(r0[:], dev[:]))
                link(v.scalar_tensor_tensor(out=nb0[:], in0=gm0[:], scalar=-1.0, in1=r0[:], op0=ALU.mult, op1=ALU.mult))

        with ExitStack() as ph:
            def ps_(name, shape):
                return ph.enter_context(nc.psum_tensor(name, shape, F32))

            def sem_(name):
                return ph.enter_context(nc.semaphore(name))

            def sb_(name, shape):
                return ph.enter_context(nc.sbuf_tensor(name, shape, F32))

            QR = C + NH
            wq_sb = sb_("wq_sb", [C, C])
            wkv_sb = sb_("wkv_sb", [C, 2 * C])
            wp_sb = sb_("wp_sb", [C, C])
            head96_sb = sb_("head96_sb", [QR, C])
            head8_sb = sb_("head8_sb", [QR, NH])
            keps_sb = sb_("keps_sb", [QR, 1])
            xn = sb_("xn", [C, 4, TOK])
            q_sb = sb_("q_sb", [QR, 2, TOK])
            qsq = sb_("qsq", [C, TOK])
            ksq = sb_("ksq", [128, TG * C])
            knorm = sb_("knorm", [128, 3, TG * NH])
            khat = sb_("khat", [128, TG, QR])
            v_sb = sb_("v_sb", [128, TG, C + 1])
            kv_sb = sb_("kv_sb", [QR, 2, C])
            den_w = sb_("den_w", [QR, 2, NH])
            rden = sb_("rden", [128, TG * NH])
            rden_x = sb_("rden_x", [128, TG, C])
            rb_sb = sb_("rb_sb", [C, TOK])
            att = sb_("att", [C, TOK])
            yt = sb_("yt", [C, 2, TOK])
            junk = sb_("junk", [C, TOK])
            cxy8 = sb_("cxy8", [C, 2, PAIRS])

            ps_q = ps_("ps_q", [C, TOK])
            ps_kv = ps_("ps_kv", [128, TG, 256])
            ps_qn = ps_("ps_qn", [128, TOK])
            ps_g = ps_("ps_g", [128, 512])
            ps_num = ps_("ps_num", [C, TOK])
            ps_rb = ps_("ps_rb", [C, TOK])
            ps_y = ps_("ps_y", [C, TOK])
            GW = C + 1
            den_at = ps_g[:, 256:256 + TG * NH]

            w_in = sem_("w_in")
            ones_set = sem_("ones_set")
            x_in = [sem_(f"xb_in{k}") for k in range(2)]
            y_stored = [sem_(f"y_stored{k}") for k in range(2)]
            xn_ready = sem_("xn_ready")
            q_ready, kv_ready = sem_("q_ready"), sem_("kv_ready")
            q_copied, qsq_ready, ksq_ready, v_copied = (sem_(n) for n in ("q_copied", "qsq_ready", "ksq_ready", "v_copied"))
            kss_ready, kn_ready, krec_ready, khat_ready = (sem_(n) for n in ("kss_ready", "kn_ready", "krec_ready", "khat_ready"))
            qss_ready, qn_ready = sem_("qss_ready"), sem_("qn_ready")
            g_ready, gm_ready = sem_("g_ready"), sem_("gm_ready")
            den_ready, rden_ready, rdenx_ready = sem_("den_ready"), sem_("rden_ready"), sem_("rdenx_ready")
            num_ready, rb_copied, att_ready = sem_("num_ready"), sem_("rb_copied"), sem_("att_ready")
            y_ready, y_copied, y_counted, xy_counted = (sem_(n) for n in ("y_ready", "y_copied", "y_counted", "xy_counted"))
            xy_summed = sem_("xy_summed")
            y_placed, pool_turn = sem_("y_placed"), sem_("pool_turn")
            block = ph.enter_context(nc.Block())

            @block.sync
            def _(sp):
                for dst, src in ((wq_sb, wq_t), (wkv_sb, wkv_t), (wp_sb, wp_t), (head96_sb, head96), (head8_sb, head8),
                                 (keps_sb, keps)):
                    sp.dma_start(dst[:], src).then_inc(w_in, 16)

                def load(n, k):
                    b, s = (n // STRIPS_IMG, n % STRIPS_IMG)
                    sp.dma_start(xs[:, k, :], x_strips[bass.ds(b, 1), bass.ds(s, 1)].squeeze()).then_inc(x_in[k], 16)

                def store(n, k):
                    b, s = (n // STRIPS_IMG, n % STRIPS_IMG)
                    sp.dma_start(y_strips[bass.ds(b, 1), bass.ds(s, 1)].squeeze(), ys[:, k, :]).then_inc(y_stored[k], 16)

                for k in range(2):
                    load(k, k)
                with sp.Fori(0, STRIPS // 2 - 1) as m:
                    for k in range(2):
                        sp.wait_ge(xn_ready, (m * 2 + k + 1) * PAIRS)
                        load(m * 2 + (k + 2), k)
                        sp.wait_ge(y_placed, (m * 2 + k + 1) * PAIRS)
                        store(m * 2 + k, k)
                for n in (STRIPS - 2, STRIPS - 1):
                    sp.wait_ge(y_placed, (n + 1) * PAIRS)
                    store(n, n % 2)
                for k in range(2):
                    sp.wait_ge(y_stored[k], 16 * STRIPS // 2)

            @block.scalar
            def _(act):
                s_ = nc.scalar

                def normalise(n, k, j):
                    u = n * PAIRS + j
                    b = n // STRIPS_IMG
                    src = xs[:, k, :].rearrange("p (r g c) -> p g r c", r=WS, c=WS)[:, 2 * j:2 * j + 2]
                    dst = xn[:, j % 4, :].rearrange("p (g r c) -> p g r c", g=2, r=WS)
                    s_.activation(dst, src, ACT.Identity, scale=r0[:, bass.ds(b, 1)], bias=nb0[:, bass.ds(b, 1)]
                                  ).then_inc(xn_ready, 1)

                def copy_y(n, j, first=False):
                    u = n * PAIRS + j
                    if not first:
                        act.wait_ge(xy_counted, u - 1)
                        act.wait_ge(y_placed, u - 1)
                    act.wait_ge(y_ready, u + 1)
                    s_.activation(yt[:, j % 2, :], ps_y[:], ACT.Copy).then_inc(y_copied, 1)

                def step(n, k, j, first=False, last=False, load_no=None):
                    u = n * PAIRS + j
                    if first and j == 0:
                        prev = None
                    else:
                        prev = (n, k, j - 1) if j else (n - 1, 1 - k, PAIRS - 1)
                    act.wait_ge(q_ready, u + 1)
                    s_.activation(q_sb[0:C, j % 2, :], ps_q[:], ACT.Copy).then_inc(q_copied, 1)
                    s_.activation(qsq[:], ps_q[:], ACT.Square).then_inc(qsq_ready, 1)
                    act.wait_ge(kv_ready, u + 1)
                    s_.activation(ksq[:].rearrange("p (g c) -> p g c", g=TG), ps_kv[:, :, 0:C], ACT.Square
                                  ).then_inc(ksq_ready, 1)
                    s_.activation(v_sb[:, :, 0:C], ps_kv[:, :, C:2 * C], ACT.Copy).then_inc(v_copied, 1)
                    act.wait_ge(kss_ready, u + 1)
                    s_.activation(knorm[:, 1, :], knorm[:, 0, :], ACT.Sqrt).then_inc(kn_ready, 1)
                    if prev:
                        act.wait_ge(num_ready, u)
                        s_.activation(rb_sb[:], ps_rb[:], ACT.Copy).then_inc(rb_copied, 1)
                    if j + 2 == PAIRS and not last:
                        act.wait_ge(x_in[1 - k], load_no)
                    if not (first and j < 2):
                        act.wait_ge(xy_counted, u - 1)
                    act.wait_ge(qss_ready, u + 1)
                    s_.activation(q_sb[C:QR, j % 2, :], ps_qn[C:QR, :], ACT.Sqrt).then_inc(qn_ready, 1)
                    if j + 2 < PAIRS:
                        normalise(n, k, j + 2)
                    elif not last:
                        normalise(n + 1, 1 - k, j + 2 - PAIRS)
                    if prev:
                        copy_y(prev[0], prev[2], first and j <= 2)

                act.wait_ge(x_in[0], 16)
                for j in range(2):
                    normalise(0, 0, j)
                for k in range(2):
                    for j in range(PAIRS):
                        step(k, k, j, first=k == 0, load_no=16 * (k + 1))
                with act.Fori(1, STRIPS // 2 - 1) as m:
                    for k in range(2):
                        for j in range(PAIRS):
                            step(m * 2 + k, k, j, load_no=(m + 1 + k) * 16)
                m = STRIPS // 2 - 1
                for k in range(2):
                    for j in range(PAIRS):
                        step(2 * m + k, k, j, last=k == 1, load_no=16 * (m + 1 + k))
                act.wait_ge(num_ready, LAST)
                s_.activation(rb_sb[:], ps_rb[:], ACT.Copy).then_inc(rb_copied, 1)
                copy_y(STRIPS - 1, PAIRS - 1)

            @block.gpsimd
            def _(pool):
                nc.gpsimd.memset(khat[:, :, C:QR], 1.0).then_inc(ones_set, 1)
                nc.gpsimd.memset(v_sb[:, :, C:C + 1], 1.0).then_inc(ones_set, 1)

                def spread(u):
                    pool.wait_ge(rden_ready, u + 1)
                    pool.sem_inc(pool_turn, 1)
                    nc.gpsimd.tensor_copy(
                        rden_x[:].rearrange("p g (h c) -> p (g h) c", h=NH),
                        rden[:].unsqueeze(2).to_broadcast([128, TG * NH, HD])).then_inc(rdenx_ready, 1)

                def place(n, k, j, stored_no=None):
                    if j == 0 and stored_no is not None:
                        pool.wait_ge(y_stored[k], stored_no)
                    pool.wait_ge(y_copied, n * PAIRS + j + 1)
                    pool.sem_inc(pool_turn, 1)
                    dst = ys[:, k, :].rearrange("p (r g c) -> p g r c", r=WS, c=WS)[:, 2 * j:2 * j + 2]
                    nc.gpsimd.tensor_copy(dst, yt[:, j % 2, :].rearrange("p (g r c) -> p g r c", g=2, r=WS)
                                          ).then_inc(y_placed, 1)

                def strips(m, stored_no=None):
                    for k in range(2):
                        for j in range(PAIRS):
                            n = m * 2 + k
                            spread(n * PAIRS + j)
                            place(n, k, j, stored_no)

                strips(0)
                with pool.Fori(1, STRIPS // 2) as m:
                    strips(m, m * 16)

            @block.tensor
            def _(pe):
                mm = nc.tensor.matmul

                def project_q(u, j, first):
                    pe.wait_ge(xn_ready, u + 1)
                    if not first:
                        pe.wait_ge(q_copied, u)
                    mm(ps_q[:], wq_sb[:], xn[:, j % 4, :], start=True, stop=True).then_inc(q_ready, 1)

                def project_kv(u, j):
                    for g in range(TG):
                        last = mm(ps_kv[:, g, 0:2 * C], xn[:, j % 4, g * 128:(g + 1) * 128], wkv_sb[:], start=True,
                                  stop=True)
                    last.then_inc(kv_ready, 1)

                def denominators(u, j):
                    pe.wait_ge(qn_ready, u + 1)
                    pe.wait_ge(gm_ready, u + 1)
                    for g in range(TG):
                        last = mm(den_at[:, g * NH:(g + 1) * NH], q_sb[:, j % 2, g * 128:(g + 1) * 128],
                                  den_w[:, g // 2, :], start=True, stop=True)
                    last.then_inc(den_ready, 1)

                def numerators(u, j):
                    for w in range(2):
                        mm(ps_num[:, w * WIN:(w + 1) * WIN], kv_sb[:, w, :], q_sb[:, j % 2, w * WIN:(w + 1) * WIN],
                           start=True, stop=True)
                    pe.wait_ge(rdenx_ready, u + 1)
                    for g in range(TG):
                        last = nc.tensor.transpose(ps_rb[:, g * 128:(g + 1) * 128], rden_x[:, g, :], ident_sb[:])
                    last.then_inc(num_ready, 1)

                def q_norms(u):
                    pe.wait_ge(qsq_ready, u + 1)
                    mm(ps_qn[C:QR, :], head8_sb[0:C, :], qsq[:], start=True, stop=True).then_inc(qss_ready, 1)

                def kv_sums(u):
                    pe.wait_ge(khat_ready, u + 1)
                    pe.wait_ge(v_copied, u + 1)
                    for g in range(TG):
                        w = g // 2
                        last = mm(ps_g[0:QR, w * GW:(w + 1) * GW], khat[:, g, :], v_sb[:, g, :], start=g % 2 == 0,
                                  stop=g % 2 == 1)
                    last.then_inc(g_ready, 1)

                def project_y(u, first):
                    pe.wait_ge(att_ready, u + 1)
                    if not first:
                        pe.wait_ge(y_copied, u)
                    mm(ps_y[:], wp_sb[:], att[:], start=True, stop=True).then_inc(y_ready, 1)

                def step(u, j, first=False):
                    prev = not (first and j == 0)
                    project_q(u, j, not prev)
                    if prev:
                        denominators(u - 1, j - 1)
                    project_kv(u, j)
                    if prev:
                        numerators(u - 1, j - 1)
                    q_norms(u)
                    kv_sums(u)
                    if prev:
                        project_y(u - 1, first and j == 1)

                pe.wait_ge(w_in, 96)
                pe.wait_ge(ones_set, 2)
                for j in range(PAIRS):
                    step(j, j, first=True)
                with pe.Fori(1, STRIPS) as n:
                    for j in range(PAIRS):
                        step(n * PAIRS + j, j)
                denominators(LAST - 1, PAIRS - 1)
                numerators(LAST - 1, PAIRS - 1)
                project_y(LAST - 1, False)

            @block.vector
            def _(dve):
                v = nc.vector

                def invert_den(u):
                    dve.wait_ge(den_ready, u + 1)
                    v.reciprocal(rden[:], den_at).then_inc(rden_ready, 1)

                def unit_k(u):
                    dve.wait_ge(ksq_ready, u + 1)
                    v.tensor_reduce(knorm[:, 0, :], ksq[:].rearrange("p (h c) -> p h c", c=HD), AX.X, ALU.add
                                    ).then_inc(kss_ready, 1)
                    dve.wait_ge(kn_ready, u + 1)
                    v.reciprocal(knorm[:, 2, :], knorm[:, 1, :]).then_inc(krec_ready, 1)
                    dve.wait_ge(krec_ready, u + 1)
                    v.tensor_tensor(khat[:, :, 0:C].rearrange("p g (h c) -> p g h c", c=HD),
                                    ps_kv[:, :, 0:C].rearrange("p g (h c) -> p g h c", c=HD),
                                    knorm[:, 2, :].rearrange("p (g h) -> p g h", g=TG).unsqueeze(3).to_broadcast(
                                        [128, TG, NH, HD]), ALU.mult).then_inc(khat_ready, 1)

                def attend(u):
                    dve.wait_ge(rb_copied, u + 1)
                    v.tensor_tensor(att[:], ps_num[:], rb_sb[:], ALU.mult).then_inc(att_ready, 1)

                def window_sums(u):
                    dve.wait_ge(g_ready, u + 1)
                    g = ps_g[0:QR, 0:2 * GW].rearrange("p (w c) -> p w c", w=2)
                    v.tensor_tensor(kv_sb[:], g[:, :, 0:C], head96_sb[:].unsqueeze(1).to_broadcast([QR, 2, C]), ALU.mult)
                    for w in range(2):
                        last = v.scalar_tensor_tensor(out=den_w[:, w, :], in0=g[:, w, C:C + 1].to_broadcast([QR, NH]),
                                                      scalar=keps_sb[:], in1=head8_sb[:], op0=ALU.add, op1=ALU.mult)
                    last.then_inc(gm_ready, 1)

                def count_y(u, j):
                    dve.wait_ge(y_copied, u + 1)
                    v.bn_stats(stat_y[:, bass.ds(u * STAT, STAT)], yt[:, j % 2, :]).then_inc(y_counted, 1)
                    v.tensor_tensor_reduce(out=junk[:], in0=yt[:, j % 2, :], in1=xn[:, j % 4, :], scale=1.0, scalar=0.0,
                                           op0=ALU.mult, op1=ALU.add, accum_out=cxy8[:, 0, j:j + 1]
                                           ).then_inc(xy_counted, 1)

                def sum_strip(n):
                    dve.wait_ge(xy_counted, (n + 1) * PAIRS)
                    v.tensor_reduce(cxy_strip[:, bass.ds(n, 1)], cxy8[:, 0, :], AX.X, ALU.add).then_inc(xy_summed, 1)

                def step(u, j, n, first=False):
                    prev = not (first and j == 0)
                    if prev:
                        invert_den(u - 1)
                    unit_k(u)
                    if prev:
                        attend(u - 1)
                    window_sums(u)
                    if prev:
                        count_y(u - 1, (j - 1) % PAIRS)
                        if j == 0:
                            sum_strip(n - 1)
                            dve.wait_ge(xy_summed, n)

                dve.wait_ge(w_in, 96)
                for j in range(PAIRS):
                    step(j, j, 0, first=True)
                with dve.Fori(1, STRIPS) as n:
                    for j in range(PAIRS):
                        step(n * PAIRS + j, j, n)
                invert_den(LAST - 1)
                attend(LAST - 1)
                count_y(LAST - 1, PAIRS - 1)
                sum_strip(STRIPS - 1)
                dve.wait_ge(xy_summed, STRIPS)
                dve.wait_ge(y_counted, LAST)

        with ExitStack() as ph:
            def sb_(name, shape):
                return ph.enter_context(nc.sbuf_tensor(name, shape, F32))

            def sem_(name):
                return ph.enter_context(nc.semaphore(name))

            mv = sb_("mv2", [C, B, 2])
            mean_y, var_y, cxy, mean_n = (sb_(n, [C, B]) for n in ("mean_y", "var_y", "cxy", "mean_n"))
            tmp, m1, v1, r1 = (sb_(n, [C, B]) for n in ("tmp", "m1", "v1", "r1"))
            s1 = sb_("s1", [C, 8])
            par = sb_("par", [C, NPAR])
            ps_m = ph.enter_context(nc.psum_tensor("ps_m2", [C, 512], F32))
            ps_v = ph.enter_context(nc.psum_tensor("ps_v2", [C, 512], F32))
            veps, sd, means, gmeans, vars_, gvars, par_set, par_out, chain = (
                sem_(n) for n in ("veps2", "sd2", "means2", "gmeans2", "vars2", "gvars2", "par_set", "par_out", "chain2"))
            block = ph.enter_context(nc.Block())

            @block.scalar
            def _(act):
                act.wait_ge(veps, 1)
                nc.scalar.activation(s1[:, 2:3], s1[:, 1:2], ACT.Sqrt).then_inc(sd, 1)
                act.wait_ge(veps, 2)
                nc.scalar.activation(tmp[:], v1[:], ACT.Sqrt).then_inc(sd, 1)

            @block.tensor
            def _(pe):
                pe.wait_ge(means, 1)
                nc.tensor.matmul(ps_m[:, 0:B], gmean_sb[:], m1[:], start=True, stop=True).then_inc(gmeans, 1)
                pe.wait_ge(vars_, 1)
                nc.tensor.matmul(ps_v[:, 0:B], gmean_sb[:], v1[:], start=True, stop=True).then_inc(gvars, 1)

            @block.sync
            def _(sp):
                sp.wait_ge(par_set, 1)
                sp.dma_start(par_dram, par[:]).then_inc(par_out, 16)
                sp.wait_ge(par_out, 16)

            @block.vector
            def _(dve):
                v = nc.vector
                steps = [0]

                def link(ins):
                    steps[0] += 1
                    ins.then_inc(chain, 1)
                    dve.wait_ge(chain, steps[0])

                def tt(o, a, b, op):
                    link(v.tensor_tensor(o, a, b, op))

                n_img = float(H * W)
                for b in range(B):
                    last = v.bn_aggr(mv[:, b, :], stat_y[:, b * 128 * STAT:(b + 1) * 128 * STAT])
                link(last)
                v.tensor_copy(mean_y[:], mv[:, :, 0])
                link(v.tensor_copy(var_y[:], mv[:, :, 1]))
                link(v.tensor_reduce(s1[:, 0:1], mean_y[:], AX.X, ALU.add))
                link(v.tensor_scalar(s1[:, 0:1], s1[:, 0:1], 1.0 / B, None, ALU.mult))
                link(v.tensor_scalar(tmp[:], mean_y[:], s1[:, 0:1], None, ALU.subtract))
                tt(tmp[:], tmp[:], tmp[:], ALU.mult)
                tt(tmp[:], tmp[:], var_y[:], ALU.add)
                link(v.tensor_reduce(s1[:, 1:2], tmp[:], AX.X, ALU.add))
                link(v.tensor_scalar(s1[:, 1:2], s1[:, 1:2], 1.0 / B, BN_EPS, ALU.mult, ALU.add))
                dve.sem_inc(veps, 1)
                dve.wait_ge(sd, 1)
                link(v.reciprocal(s1[:, 3:4], s1[:, 2:3]))
                tt(s1[:, 4:5], s1[:, 3:4], gb[:, 0:1], ALU.mult)
                tt(s1[:, 5:6], s1[:, 0:1], s1[:, 4:5], ALU.mult)
                tt(s1[:, 5:6], gb[:, 1:2], s1[:, 5:6], ALU.subtract)
                link(v.tensor_reduce(cxy[:], cxy_strip[:].rearrange("p (b s) -> p b s", b=B), AX.X, ALU.add))
                tt(mean_n[:], mean_x[:], gm0[:], ALU.subtract)
                tt(mean_n[:], mean_n[:], r0[:], ALU.mult)
                tt(mean_n[:], mean_n[:], mean_y[:], ALU.mult)
                link(v.scalar_tensor_tensor(out=cxy[:], in0=cxy[:], scalar=1.0 / n_img, in1=mean_n[:], op0=ALU.mult,
                                            op1=ALU.subtract))
                link(v.reciprocal(tmp[:], r0[:]))
                tt(cxy[:], cxy[:], tmp[:], ALU.mult)
                link(v.scalar_tensor_tensor(out=m1[:], in0=mean_y[:], scalar=s1[:, 4:5], in1=mean_x[:], op0=ALU.mult,
                                            op1=ALU.add))
                link(v.tensor_scalar(m1[:], m1[:], s1[:, 5:6], None, ALU.add))
                dve.sem_inc(means, 1)
                link(v.tensor_scalar(tmp[:], var_y[:], s1[:, 4:5], None, ALU.mult))
                link(v.scalar_tensor_tensor(out=tmp[:], in0=cxy[:], scalar=2.0, in1=tmp[:], op0=ALU.mult, op1=ALU.add))
                link(v.scalar_tensor_tensor(out=v1[:], in0=tmp[:], scalar=s1[:, 4:5], in1=var_x[:], op0=ALU.mult,
                                            op1=ALU.add))
                dve.wait_ge(gmeans, 1)
                tt(tmp[:], m1[:], ps_m[:, 0:B], ALU.subtract)
                link(v.tensor_copy(m1[:], ps_m[:, 0:B]))
                tt(tmp[:], tmp[:], tmp[:], ALU.mult)
                tt(v1[:], v1[:], tmp[:], ALU.add)
                dve.sem_inc(vars_, 1)
                dve.wait_ge(gvars, 1)
                link(v.tensor_scalar(v1[:], ps_v[:, 0:B], GN_EPS, None, ALU.add))
                dve.sem_inc(veps, 1)
                dve.wait_ge(sd, 2)
                link(v.reciprocal(r1[:], tmp[:]))
                link(v.tensor_scalar(tmp[:], m1[:], s1[:, 5:6], -1.0, ALU.subtract, ALU.mult))
                tt(par[:, 2 + B:2 + 2 * B], tmp[:], r1[:], ALU.mult)
                link(v.tensor_copy(par[:, 2:2 + B], r1[:]))
                link(v.tensor_copy(par[:, 0:1], s1[:, 4:5]))
                tt(par[:, 1:2], s1[:, 5:6], gb[:, 2:3], ALU.add)
                dve.sem_inc(par_set, 1)

        with ExitStack() as ph:
            def ps_(name, shape):
                return ph.enter_context(nc.psum_tensor(name, shape, F32))

            def sem_(name):
                return ph.enter_context(nc.semaphore(name))

            def sb_(name, shape):
                return ph.enter_context(nc.sbuf_tensor(name, shape, F32))

            GP = C * SETS
            XN = PAIRW * IMGS * W
            x1, yb, ob = ([arena[:, (SETS * a + g) * XN:(SETS * a + g + 1) * XN].rearrange(
                "p (i b w) -> p i b w", i=PAIRW, b=IMGS) for g in range(SETS)] for a in range(3))
            ZN = WINDOWS * IMGS * ZW
            zb = [arena[:, 6 * XN + g * ZN:6 * XN + (g + 1) * ZN].rearrange("p (t b w) -> p t b w", t=WINDOWS, b=IMGS)
                  for g in range(SETS)]
            assert 6 * XN + 2 * ZN <= 31232
            raw1 = sb_("raw1", [128, 2 * TAPS, WROWS])
            raw2 = sb_("raw2", [128, 2 * TAPS, HALF])
            raw3 = sb_("raw3", [128, 2 * TAPS, HALF])
            mat1 = [sb_(f"mat1_{k}", [128, TAPS, 2 * WROWS]) for k in range(2)]
            mat2 = [sb_(f"mat2_{k}", [128, 2, TAPS, HALF]) for k in range(2)]
            mat3 = [sb_(f"mat3_{k}", [128, 2, TAPS, HALF]) for k in range(2)]
            prm = [sb_(f"prm_{k}", [128, NPAR]) for k in range(2)]
            shift = [sb_(f"shift_{k}", [128, PAIRW, B]) for k in range(2)]
            down_sb = sb_("down_sb", [128, WINDOWS, HALF])
            up_sb = sb_("up_sb", [128, WINDOWS, 2 * WROWS])
            inside_sb = sb_("inside_sb", [128, PAIRW])
            ll1 = sb_("ll1", [128, IMGS, HALF])
            in2 = sb_("in2", [128, 2, IMGS, HALF // 2 + 4])
            in3 = sb_("in3", [128, 2, IMGS, HALF // 4 + 4])
            s3 = sb_("s3", [128, IMGS * HALF // 4])
            up3 = sb_("up3", [128, IMGS * HALF // 4, 2])
            low2 = sb_("low2", [128, IMGS * HALF // 2])
            next_ll = sb_("next_ll", [128, IMGS * HALF // 2, 2])
            ps_w = [ps_(f"ps_w{t}", [128, IMGS * HALF]) for t in range(WINDOWS)]
            ps_ll = ps_("ps_ll", [128, IMGS * HALF])
            ps_2 = ps_("ps_2", [128, 2, IMGS * HALF // 2])
            ps_3 = ps_("ps_3", [128, 2, 256])

            prm_in = [sem_(f"prm_in{k}") for k in range(2)]
            pool_turn = sem_("pool_turn_c")
            raw_in, mats_ready = sem_("raw_in"), sem_("mats_ready")
            const_in, zeroed = sem_("constc_in"), sem_("zeroed")
            xy_in = [sem_(f"xy_in{g}") for g in range(SETS)]
            x1_ready, shift_ready, z_act, z_dve = (sem_(n) for n in ("x1_ready", "shift_ready", "z_act", "z_dve"))
            ll_ready, ll_copied, in2_ready, in3_ready = (sem_(n) for n in ("ll_ready", "ll_copied", "in2_ready", "in3_ready"))
            l3_ready, s3_copied, up3_ready, l2_ready, low2_ready, next_ready = (
                sem_(n) for n in ("l3_ready", "s3_copied", "up3_ready", "l2_ready", "low2_ready", "next_ready"))
            win_ready = sem_("win_ready")
            out_ready = sem_("out_ready")
            LEAD = 3 * WINDOWS
            stored = [sem_(f"stored{g}") for g in range(SETS)]
            block = ph.enter_context(nc.Block())
            NLOAD = 2 * WINDOWS * 16
            NRAW = (4 + 2 + 4) * 16

            def zero_pads(eng):
                for g in range(SETS):
                    eng.memset(x1[g], 0.0).then_inc(zeroed, 1)
                    eng.memset(yb[g], 0.0).then_inc(zeroed, 1)
                    eng.memset(zb[g], 0.0).then_inc(zeroed, 1)
                eng.memset(in2[:], 0.0).then_inc(zeroed, 1)
                eng.memset(in3[:], 0.0).then_inc(zeroed, 1)

            N_ZERO = 3 * SETS + 2

            @block.sync
            def _(sp):
                for dst, src in ((down_sb, down), (up_sb, up), (inside_sb, inside)):
                    sp.dma_start(dst[:], src).then_inc(const_in, 16)

                def load_prm(c, k):
                    sp.dma_start(prm[k][:], bass.AP(tensor=par_dram.tensor, offset=c * NPAR, ap=[[0, 128], [1, NPAR]])
                                 ).then_inc(prm_in[k], 16)

                def load_raw(c):
                    for ia in range(2):
                        for q in range(2):
                            first = q * WROWS + ia
                            sp.dma_start(raw1[first:first + WROWS - 1:2, :, :],
                                         bass.AP(tensor=vec1.tensor,
                                                 offset=c * (NV1 * V1) + ((2 * ia + q) * 2 * TAPS * V1 + 2),
                                                 ap=[[2, WROWS // 2], [V1, 2 * TAPS], [1, WROWS]])).then_inc(raw_in, 16)
                    for ia in range(2):
                        sp.dma_start(raw2[ia:128:2, :, :],
                                     bass.AP(tensor=vec2.tensor, offset=c * (NV2 * V2) + (ia * 2 * TAPS * V2 + 2),
                                             ap=[[2, HALF // 2], [V2, 2 * TAPS], [1, HALF]])).then_inc(raw_in, 16)
                    for rho in range(4):
                        sp.dma_start(raw3[rho:128:4, :, :],
                                     bass.AP(tensor=vec3.tensor,
                                             offset=c * (NV2 * V2) + (rho // 2 * 2 * TAPS * V2 + 4),
                                             ap=[[4, HALF // 4], [V2, 2 * TAPS], [1, HALF]])).then_inc(raw_in, 16)

                def load_xy(c, g):
                    for t in range(WINDOWS):
                        lo, hi, skip = window_rows(t)
                        p = (t % 2) * WROWS + skip
                        for dst, src in ((x1[g], x), (yb[g], y_dram)):
                            sp.dma_start(dst[p:p + hi - lo, t // 2],
                                         src[IMGS * g:IMGS * (g + 1), bass.ds(c, 1), lo:hi, :].rearrange(
                                             "b o h w -> (o h) b w")).then_inc(xy_in[g], 16)

                def store(c, g, count):
                    for t in range(WINDOWS):
                        sp.wait_ge(out_ready, count * WINDOWS + (LEAD + t + 1))
                        n = min(OROWS, H - OROWS * t)
                        p = (t % 2) * WROWS + HALO
                        sp.dma_start(out[IMGS * g:IMGS * (g + 1), bass.ds(c, 1), OROWS * t:OROWS * t + n, :].rearrange(
                            "b o h w -> (o h) b w"), ob[g][p:p + n, t // 2]).then_inc(stored[g], 16)

                sp.wait_ge(zeroed, N_ZERO)
                load_raw(0)
                for g in range(SETS):
                    sp.sem_inc(stored[g], 16)
                for k in range(2):
                    load_prm(k, k)
                for g in range(SETS):
                    load_xy(0, g)
                sp.wait_ge(mats_ready, 1)
                load_raw(1)
                with sp.Fori(0, C // 2 - 1) as m:
                    for k in range(2):
                        for g in range(SETS):
                            store(m * 2 + k, g, m * 4 + (2 * k + g))
                            load_xy(m * 2 + (k + 1), g)
                            if g == 0:
                                sp.wait_ge(mats_ready, m * 2 + (k + 2))
                                load_raw(m * 2 + (k + 2))
                        load_prm(m * 2 + (k + 2), k)
                for k in range(2):
                    for g in range(SETS):
                        store(C - 2 + k, g, 2 * (C - 2 + k) + g)
                        if k == 0:
                            load_xy(C - 1, g)
                for g in range(SETS):
                    sp.wait_ge(stored[g], 16 * WINDOWS * C + 16)

            @block.gpsimd
            def _(pool):
                zero_pads(nc.gpsimd)
                with pool.Fori(0, C // 2) as m:
                    for k in range(2):
                        pool.wait_ge(raw_in, m * (2 * NRAW) + (k + 1) * NRAW)
                        pool.wait_ge(out_ready, m * (4 * WINDOWS) + (2 * k - 2) * WINDOWS + LEAD)
                        pool.sem_inc(pool_turn, 1)
                        nc.gpsimd.tensor_copy(mat1[k][:],
                                              raw1[:].rearrange("p (d o) m -> p d (o m)", o=2)[:, :, ::-1])
                        nc.gpsimd.tensor_copy(mat2[k][:].rearrange("p s d m -> p (s d) m"), raw2[:, :, ::-1])
                        nc.gpsimd.tensor_copy(mat3[k][:].rearrange("p s d m -> p (s d) m"), raw3[:, :, ::-1]
                                              ).then_inc(mats_ready, 1)

            def group_loop(eng, body):
                with eng.Fori(0, C // 2) as m:
                    for k in range(2):
                        for g in range(SETS):
                            body(m * 4 + (2 * k + g), m, k, g)

            def z_ops(eng_op, k, g, t, q):
                p = (t % 2) * WROWS
                for b in range(IMGS):
                    img = IMGS * g + b
                    last = eng_op(zb[g][q * WROWS:(q + 1) * WROWS, t, b, 2:2 + HALF],
                                  x1[g][p:p + WROWS, t // 2, b, q::2],
                                  prm[k][p:p + WROWS, 2 + img:3 + img], shift[k][p:p + WROWS, t // 2, img:img + 1])
                return last

            @block.scalar
            def _(act):
                def norm(o, i, scale, bias):
                    return nc.scalar.activation(o, i, ACT.Identity, scale=scale, bias=bias)

                def body(qn, m, k, g):
                    act.wait_ge(x1_ready, (qn + 1) * PAIRW)
                    act.wait_ge(shift_ready, m * 2 + k + 1)
                    for t in range(WINDOWS):
                        z_ops(norm, k, g, t, 0).then_inc(z_act, 1)
                    act.wait_ge(ll_ready, qn + 1)
                    nc.scalar.activation(ll1[:].rearrange("p b w -> p (b w)"), ps_ll[:], ACT.Copy).then_inc(ll_copied, 1)
                    act.wait_ge(l3_ready, qn + 1)
                    nc.scalar.activation(s3[:], ps_3[:, 0, 0:IMGS * HALF // 4], ACT.Copy).then_inc(s3_copied, 1)

                group_loop(act, body)

            @block.tensor
            def _(pe):
                mm = nc.tensor.matmul

                def body(qn, m, k, g):
                    pe.wait_ge(z_act, (qn + 1) * WINDOWS)
                    pe.wait_ge(z_dve, (qn + 1) * WINDOWS)
                    for t in range(WINDOWS):
                        last = mm(ps_ll[:], down_sb[:, t, :], zb[g][:, t, :, 2:2 + HALF], start=t == 0,
                                  stop=t == WINDOWS - 1)
                    last.then_inc(ll_ready, 1)
                    pe.wait_ge(mats_ready, m * 2 + k + 1)

                    def conv(t):
                        pe.wait_ge(out_ready, qn * WINDOWS + (LEAD + t + 1 - WINDOWS))
                        for d in range(TAPS):
                            mm(ps_w[t][:], mat1[k][:, d, :], zb[g][:, t, :, d:d + HALF], start=d == 0, stop=False)

                    def level(ps, mat, src, n):
                        for s in range(2):
                            for d in range(TAPS):
                                last = mm(ps[:, s, 0:IMGS * n], mat[k][:, s, d, :], src[:, s, :, d:d + n],
                                          start=d == 0, stop=d == TAPS - 1)
                        return last

                    conv(0)
                    conv(1)
                    pe.wait_ge(in3_ready, qn + 1)
                    level(ps_3, mat3, in3, HALF // 4).then_inc(l3_ready, 1)
                    level(ps_2, mat2, in2, HALF // 2).then_inc(l2_ready, 1)
                    for t in range(2, WINDOWS):
                        conv(t)
                    pe.wait_ge(next_ready, qn + 1)
                    for t in range(WINDOWS):
                        mm(ps_w[t][:], up_sb[:, t, :], next_ll[:].rearrange("p n c -> p (n c)"), start=False, stop=True
                           ).then_inc(win_ready, 1)

                pe.wait_ge(const_in, 48)
                pe.wait_ge(zeroed, N_ZERO)
                group_loop(pe, body)

            @block.vector
            def _(dve):
                v = nc.vector

                def norm(o, i, scale, bias):
                    return v.tensor_scalar(o, i, scale, bias, ALU.mult, ALU.add)

                def prepare(qn, m, k, g):
                    if g == 0:
                        dve.wait_ge(prm_in[k], m * 16 + 16)
                        v.tensor_tensor(shift[k][:], prm[k][:, 2 + B:2 + 2 * B].unsqueeze(1).to_broadcast([128, PAIRW, B]),
                                        inside_sb[:].unsqueeze(2).to_broadcast([128, PAIRW, B]), ALU.mult
                                        ).then_inc(shift_ready, 1)
                    dve.wait_ge(xy_in[g], (m * 2 + k + 1) * NLOAD)
                    for i in range(PAIRW):
                        n = 128 if 2 * i + 1 < WINDOWS else WROWS
                        v.scalar_tensor_tensor(out=x1[g][0:n, i].rearrange("p b w -> p (b w)"),
                                               in0=yb[g][0:n, i].rearrange("p b w -> p (b w)"), scalar=prm[k][0:n, 0:1],
                                               in1=x1[g][0:n, i].rearrange("p b w -> p (b w)"), op0=ALU.mult, op1=ALU.add
                                               ).then_inc(x1_ready, 1)
                    dve.wait_ge(shift_ready, m * 2 + k + 1)
                    dve.wait_ge(x1_ready, (qn + 1) * PAIRW)
                    for t in range(WINDOWS):
                        z_ops(norm, k, g, t, 1).then_inc(z_dve, 1)

                def low_levels(qn):
                    dve.wait_ge(ll_copied, qn + 1)
                    for s, op in enumerate((ALU.add, ALU.subtract)):
                        v.tensor_tensor(in2[:, s, :, 2:2 + HALF // 2], ll1[:, :, 0::2], ll1[:, :, 1::2], op
                                        ).then_inc(in2_ready, 1)
                    dve.wait_ge(in2_ready, 2 * qn + 2)
                    for s, op in enumerate((ALU.add, ALU.subtract)):
                        last = v.tensor_tensor(in3[:, s, :, 2:2 + HALF // 4], in2[:, 0, :, 2:2 + HALF // 2:2],
                                               in2[:, 0, :, 3:2 + HALF // 2:2], op)
                    last.then_inc(in3_ready, 1)
                    n = IMGS * HALF // 4
                    dve.wait_ge(s3_copied, qn + 1)
                    v.tensor_tensor(up3[:, :, 0], s3[:], ps_3[:, 1, 0:n], ALU.add)
                    v.tensor_tensor(up3[:, :, 1], s3[:], ps_3[:, 1, 0:n], ALU.subtract).then_inc(up3_ready, 1)
                    dve.wait_ge(l2_ready, qn + 1)
                    dve.wait_ge(up3_ready, qn + 1)
                    v.tensor_tensor(low2[:], up3[:].rearrange("p n c -> p (n c)"), ps_2[:, 0, :], ALU.add
                                    ).then_inc(low2_ready, 1)
                    dve.wait_ge(low2_ready, qn + 1)
                    v.tensor_tensor(next_ll[:, :, 0], low2[:], ps_2[:, 1, :], ALU.add)
                    v.tensor_tensor(next_ll[:, :, 1], low2[:], ps_2[:, 1, :], ALU.subtract).then_inc(next_ready, 1)

                def finish(qn, m, k, g, stored_no):
                    for t in range(WINDOWS):
                        p = (t % 2) * WROWS
                        dve.wait_ge(win_ready, qn * WINDOWS + t + 1)
                        if t == 0:
                            dve.wait_ge(stored[g], stored_no)
                        for q in range(2):
                            last = v.scalar_tensor_tensor(
                                out=ob[g][p:p + WROWS, t // 2].rearrange("p b w -> p (b w)")[:, q::2],
                                in0=ps_w[t][q * WROWS:(q + 1) * WROWS, :], scalar=prm[k][p:p + WROWS, 1:2],
                                in1=x1[g][p:p + WROWS, t // 2].rearrange("p b w -> p (b w)")[:, q::2],
                                op0=ALU.add, op1=ALU.add)
                        last.then_inc(out_ready, 1)

                dve.wait_ge(const_in, 48)
                dve.wait_ge(zeroed, N_ZERO)
                dve.sem_inc(out_ready, LEAD)
                prepare(0, 0, 0, 0)

                def steps(m, ks):
                    for k, g in ks:
                        qn = m * 4 + (2 * k + g)
                        low_levels(qn)
                        k2, g2 = (k, 1) if g == 0 else (1 - k, 0)
                        m2 = m + 1 if (k, g) == (1, 1) else m
                        if not (isinstance(m, int) and (m, k, g) == (C // 2 - 1, 1, 1)):
                            prepare(qn + 1, m2, k2, g2)
                        finish(qn, m, k, g, (m * 2 + k) * (16 * WINDOWS) + 16)

                ALL = [(k, g) for k in range(2) for g in range(SETS)]
                with dve.Fori(0, C // 2 - 1) as m:
                    steps(m, ALL)
                steps(C // 2 - 1, ALL)


def kernel(**inputs):
    import numpy as np
    import concourse.bacc as bacc
    from concourse.bass_utils import run_bass_kernel_spmd

    a = {k: np.ascontiguousarray(v) for k, v in inputs.items()}
    f = np.float32
    heads = np.repeat(np.arange(NH), HD)
    same = (heads[:, None] == heads[None, :]).astype(f)
    own = (np.arange(NH)[:, None] == heads[None, :]).astype(f)
    head96 = np.concatenate([same, own], 0)
    head8 = np.concatenate([own.T, np.eye(NH, dtype=f)], 0)
    keps = np.concatenate([np.full((C, 1), K_EPS, f), np.zeros((NH, 1), f)], 0)
    per = C // GROUPS
    grp = np.arange(C) // per
    gmean = (grp[:, None] == grp[None, :]).astype(f) / f(per)
    down = np.zeros((128, WINDOWS, HALF), f)
    for t in range(WINDOWS):
        for q in range(2):
            for r in range(HALO, HALO + OROWS):
                row = OROWS * t - HALO + r
                if row < H:
                    down[q * WROWS + r, t, row // 2] = 0.5
    up = np.ascontiguousarray(down.transpose(2, 1, 0))
    inside = np.zeros((128, PAIRW), f)
    for t in range(WINDOWS):
        lo, hi, skip = window_rows(t)
        inside[(t % 2) * WROWS + skip:(t % 2) * WROWS + skip + hi - lo, t // 2] = 1.0

    wqkv = a["L0_conv_w_qkv"]
    feeds = {
        "x": a["x"],
        "wq_t": wqkv[0:C].T, "wkv_t": wqkv[C:3 * C].T, "wp_t": a["L0_conv_w_proj"].T,
        "gamma": a["L0_conv_gamma"].reshape(C, 1), "beta": a["L0_conv_beta"].reshape(C, 1),
        "base_w": a["L1_conv_base_w"].reshape(C, TAPS * TAPS), "base_b": a["L1_conv_base_b"].reshape(C, 1),
        "base_scale": a["L1_conv_base_scale"].reshape(C, 1),
        "wconv": a["L1_conv_wconv_w"].reshape(3, C, 4, TAPS * TAPS).transpose(1, 0, 2, 3),
        "wscale": a["L1_conv_wscale"].reshape(3, C, 4).transpose(1, 0, 2),
        "ident": np.eye(128, dtype=f), "gmean": gmean, "head96": head96, "head8": head8, "keps": keps,
        "down": down, "up": up, "inside": inside,
    }
    feeds = {k: np.ascontiguousarray(v) for k, v in feeds.items()}
    nc = bacc.Bacc("TRN2", target_bir_lowering=False, num_devices=1)
    args = [nc.dram_tensor(f"in_{k}", v.shape, mybir.dt.from_np(v.dtype), kind="ExternalInput").ap()
            for k, v in feeds.items()]
    out = nc.dram_tensor("out_0", (B, C, H, W), F32, kind="ExternalOutput").ap()
    wt_attention_kernel(nc, *args, out)
    r = run_bass_kernel_spmd(nc, [{f"in_{k}": v for k, v in feeds.items()}], core_ids=[0])
    return r.results[0]["out_0"]
```

```python
from contextlib import ExitStack

import concourse.bass as bass
from concourse import mybir

F32 = mybir.dt.float32
F32R = mybir.dt.float32r
ALU = mybir.AluOpType
ACT = mybir.ActivationFunctionType
AX = mybir.AxisListType

B, C, H, W = 8, 96, 256, 256
WS, NH = 16, 8
HD = C // NH
GROUPS = 32
ROWS_STRIP = WS
STRIPS_IMG = H // ROWS_STRIP
STRIPS = B * STRIPS_IMG
STRIP = ROWS_STRIP * W
PAIRS = W // WS // 2
WIN = WS * WS
TOK = 2 * WIN
TG = TOK // 128
LAST = STRIPS * PAIRS
STAT = 6
GN_EPS, BN_EPS, K_EPS = 1e-5, 1e-5, 1e-6

TAPS = 5
HALF = W // 2
WROWS = 64
HALO = 4
OROWS = 52
WINDOWS = -(-H // OROWS)
PAIRW = -(-WINDOWS // 2)
IMGS = 4
SETS = B // IMGS
ZW = HALF + 4
V1 = 2 * WROWS
V2 = 2 * HALF
NV1 = 4 * TAPS * 2
NV2 = 2 * 2 * TAPS
NPAR = 2 + 2 * B


def window_rows(t):
    start = OROWS * t - HALO
    lo, hi = max(0, start), min(H, start + WROWS)
    return lo, hi, lo - start


def wt_attention_kernel(nc, x, wqkv_t, wp_t, gamma, beta, base_w, base_b, base_scale, wconv, wscale,
                        ident, gmean, head96, head8, keps, down, up, inside, out):
    y_dram = nc.dram_tensor("y_scratch", [B, C, H, W], F32, kind="Internal").ap()
    vec1 = nc.dram_tensor("vec1", [C, NV1 * V1], F32, kind="Internal").ap()
    vec2 = nc.dram_tensor("vec2", [C, NV2 * V2], F32, kind="Internal").ap()
    vec3 = nc.dram_tensor("vec3", [C, NV2 * V2], F32, kind="Internal").ap()
    par_dram = nc.dram_tensor("params", [C, NPAR], F32, kind="Internal").ap()
    x_strips = x.rearrange("b c (s r) w -> b s c (r w)", r=ROWS_STRIP)
    y_strips = y_dram.rearrange("b c (s r) w -> b s c (r w)", r=ROWS_STRIP)

    with ExitStack() as ctx:
        def sb(name, shape):
            return ctx.enter_context(nc.sbuf_tensor(name, shape, F32))

        def sem(name):
            return ctx.enter_context(nc.semaphore(name))

        ident_sb = sb("ident_sb", [128, 128])
        gmean_sb = sb("gmean_sb", [C, C])
        mean_x = sb("mean_x", [C, B])
        var_x = sb("var_x", [C, B])
        gm0 = sb("gm0", [C, B])
        r0 = sb("r0", [C, B])
        nb0 = sb("nb0", [C, B])
        cxy_strip = sb("cxy_strip", [C, STRIPS])
        gb = sb("gb", [C, 4])

        with ExitStack() as ph:
            xs = ph.enter_context(nc.sbuf_tensor("xs0", [C, 2, STRIP], F32))
            stat_x = ph.enter_context(nc.sbuf_tensor("stat_x", [C, B, 128 * STAT], F32))
            pads = ph.enter_context(nc.sbuf_tensor("pads", [C, NV1 * V1 + 2 * NV2 * V2], F32))
            pad1 = pads[:, 0:NV1 * V1]
            pad2 = pads[:, NV1 * V1:NV1 * V1 + NV2 * V2]
            pad3 = pads[:, NV1 * V1 + NV2 * V2:NV1 * V1 + 2 * NV2 * V2]

            def ps_(name, shape):
                return ph.enter_context(nc.psum_tensor(name, shape, F32))

            def sem_(name):
                return ph.enter_context(nc.semaphore(name))

            def sb_(name, shape):
                return ph.enter_context(nc.sbuf_tensor(name, shape, F32))

            taps_b = sb_("taps_b", [C, TAPS * TAPS])
            taps_w = sb_("taps_w", [C, 3, 4, TAPS * TAPS])
            scale_w = sb_("scale_w", [C, 3, 4])
            scale_q = sb_("scale_q", [C, 3, 4])
            taps_s = sb_("taps_s", [C, 3, 4, TAPS * TAPS])
            sum_t = sb_("sum_t", [C, 3, 2, 2, TAPS * TAPS])
            full1 = sb_("full1", [C, 2, 2, TAPS, TAPS])
            base_t = sb_("base_t", [C, TAPS, TAPS])
            mv = sb_("mv", [C, B, 2])
            dev = sb_("dev", [C, B])
            tot = sb_("tot", [C, B])
            ps_m = ps_("ps_m", [C, 512])
            ps_v = ps_("ps_v", [C, 512])
            const_in = sem_("const_in")
            taps_in = sem_("taps_in")
            x_in = [sem_(f"x_in{k}") for k in range(2)]
            x_used = [sem_(f"x_used{k}") for k in range(2)]
            padded = sem_("padded")
            vec_out = sem_("vec_out")
            means = sem_("means")
            gmeans = sem_("gmeans")
            vars_ = sem_("vars")
            gvars = sem_("gvars")
            veps = sem_("veps")
            sd = sem_("sd")
            chain_p = sem_("chain_p")
            chain_v = sem_("chain_v")
            block = ph.enter_context(nc.Block())

            @block.sync
            def _(sp):
                with sp.Fori(0, B) as b:
                    with sp.Fori(0, STRIPS_IMG // 2) as h:
                        for k in range(2):
                            sp.wait_ge(x_used[k], b * (STRIPS_IMG // 2) + h + 1)
                            sp.dma_start(xs[:, k, :], x_strips[bass.ds(b, 1), bass.ds(h * 2 + k, 1)].squeeze()
                                         ).then_inc(x_in[k], 16)

            @block.scalar
            def _(act):
                act.dma_start(taps_b[:], base_w).then_inc(taps_in, 16)
                act.dma_start(taps_w[:], wconv).then_inc(taps_in, 16)
                act.dma_start(scale_w[:], wscale).then_inc(taps_in, 16)
                for i, v in enumerate((gamma, beta, base_b, base_scale)):
                    act.dma_start(gb[:, i:i + 1], v).then_inc(taps_in, 16)
                act.dma_start(ident_sb[:], ident).then_inc(const_in, 16)
                act.dma_start(gmean_sb[:], gmean).then_inc(const_in, 16)
                act.wait_ge(padded, 1)
                act.dma_start(vec1, pad1).then_inc(vec_out, 16)
                act.dma_start(vec2, pad2).then_inc(vec_out, 16)
                act.dma_start(vec3, pad3).then_inc(vec_out, 16)
                act.wait_ge(veps, 1)
                nc.scalar.activation(dev[:], tot[:], ACT.Sqrt).then_inc(sd, 1)
                act.wait_ge(vec_out, 48)

            @block.gpsimd
            def _(pool):
                steps = [0]

                def link(ins):
                    steps[0] += 1
                    ins.then_inc(chain_p, 1)
                    pool.wait_ge(chain_p, steps[0])

                g = nc.gpsimd
                link(g.memset(pads[:], 0.0))
                pool.wait_ge(taps_in, 16 * 7)
                for lv, f in ((0, 0.25), (1, 0.25), (2, 0.0625)):
                    link(g.tensor_scalar(scale_q[:, lv, :], scale_w[:, lv, :], f, None, ALU.mult))
                for lv in range(3):
                    for s in range(4):
                        link(g.tensor_scalar(taps_s[:, lv, s, :], taps_w[:, lv, s, :], scale_q[:, lv, s:s + 1], None,
                                             ALU.mult))
                for lv in range(3):
                    for ab in range(2):
                        for u in range(2):
                            link(g.tensor_tensor(sum_t[:, lv, ab, u, :], taps_s[:, lv, ab, :], taps_s[:, lv, ab + 2, :],
                                                 ALU.subtract if u else ALU.add))
                for u in range(2):
                    for v in range(2):
                        link(g.tensor_tensor(full1[:, u, v].rearrange("p a b -> p (a b)"), sum_t[:, 0, 0, u, :],
                                             sum_t[:, 0, 1, u, :], ALU.subtract if v else ALU.add))
                link(g.tensor_scalar(base_t[:].rearrange("p a b -> p (a b)"), taps_b[:], gb[:, 3:4], None, ALU.mult))
                p1 = pad1.rearrange("p (ia q dj o n) -> p ia q dj o n", ia=2, q=2, dj=TAPS, o=2)
                for ia in range(2):
                    for q in range(2):
                        for oa in range(2):
                            for p in range(2):
                                o = 1 - p
                                first = WROWS - 3 - oa
                                full = p1[:, ia, q, :, o, first:first + 2 * TAPS - 1:2]
                                link(g.tensor_copy(full, full1[:, (ia + oa) % 2, (q + p) % 2].rearrange("p di dj -> p dj di")))
                                dis = [k for k in range(TAPS) if 0 <= 2 * k + ia - oa - 2 < TAPS]
                                djs = [k for k in range(TAPS) if 0 <= 2 * k + q - p - 2 < TAPS]
                                r_, c_ = 2 * dis[0] + ia - oa - 2, 2 * djs[0] + q - p - 2
                                for n, dj in enumerate(djs):
                                    lo = first + 2 * dis[0]
                                    part = p1[:, ia, q, dj, o, lo:lo + 2 * len(dis) - 1:2]
                                    link(g.tensor_tensor(part, part, base_t[:, r_:r_ + 2 * len(dis) - 1:2, c_ + 2 * n],
                                                         ALU.add))
                p2 = pad2.rearrange("p (ia ab dj n) -> p ia ab dj n", ia=2, ab=2, dj=TAPS)
                p3 = pad3.rearrange("p (ia ab dj n) -> p ia ab dj n", ia=2, ab=2, dj=TAPS)
                for ia in range(2):
                    for ab in range(2):
                        for oa in range(2):
                            t2 = sum_t[:, 1, ab, (ia + oa) % 2, :].rearrange("p (di dj) -> p dj di", dj=TAPS)
                            first = HALF - 3 - oa
                            link(g.tensor_copy(p2[:, ia, ab, :, first:first + 2 * TAPS - 1:2], t2))
                        for rho in range(4):
                            t3 = sum_t[:, 2, ab, (ia + rho // 2) % 2, :].rearrange("p (di dj) -> p dj di", dj=TAPS)
                            first = HALF - 5 - rho
                            link(g.tensor_copy(p3[:, ia, ab, :, first:first + 4 * TAPS - 3:4], t3))
                pool.sem_inc(padded, 1)

            @block.tensor
            def _(pe):
                pe.wait_ge(const_in, 32)
                pe.wait_ge(means, 1)
                nc.tensor.matmul(ps_m[:, 0:B], gmean_sb[:], mean_x[:], start=True, stop=True).then_inc(gmeans, 1)
                pe.wait_ge(vars_, 1)
                nc.tensor.matmul(ps_v[:, 0:B], gmean_sb[:], tot[:], start=True, stop=True).then_inc(gvars, 1)

            @block.vector
            def _(dve):
                steps = [0]

                def link(ins):
                    steps[0] += 1
                    ins.then_inc(chain_v, 1)
                    dve.wait_ge(chain_v, steps[0])

                v = nc.vector
                for k in range(2):
                    dve.sem_inc(x_used[k], 1)
                stat_x_all = stat_x[:].rearrange("p b n -> p (b n)")
                with dve.Fori(0, B * STRIPS_IMG // 2) as h:
                    for k in range(2):
                        dve.wait_ge(x_in[k], (h + 1) * 16)
                        for j in range(STRIP // 512):
                            last = v.bn_stats(stat_x_all[:, bass.ds((h * 16 + (k * 8 + j)) * STAT, STAT)],
                                              xs[:, k, j * 512:(j + 1) * 512])
                        last.then_inc(x_used[k], 1)
                for k in range(2):
                    dve.wait_ge(x_used[k], STRIPS // 2 + 1)
                for b in range(B):
                    last = v.bn_aggr(mv[:, b, :], stat_x[:, b, :])
                link(last)
                v.tensor_copy(var_x[:], mv[:, :, 1])
                link(v.tensor_copy(mean_x[:], mv[:, :, 0]))
                dve.sem_inc(means, 1)
                dve.wait_ge(gmeans, 1)
                link(v.tensor_copy(gm0[:], ps_m[:, 0:B]))
                link(v.tensor_tensor(dev[:], mean_x[:], gm0[:], ALU.subtract))
                link(v.tensor_tensor(dev[:], dev[:], dev[:], ALU.mult))
                link(v.tensor_tensor(tot[:], dev[:], var_x[:], ALU.add))
                dve.sem_inc(vars_, 1)
                dve.wait_ge(gvars, 1)
                v.tensor_scalar(tot[:], ps_v[:, 0:B], GN_EPS, None, ALU.add).then_inc(veps, 1)
                dve.wait_ge(sd, 1)
                link(v.reciprocal(r0[:], dev[:]))
                link(v.scalar_tensor_tensor(out=nb0[:], in0=gm0[:], scalar=-1.0, in1=r0[:], op0=ALU.mult, op1=ALU.mult))

        until_params = ctx.enter_context(ExitStack())
        stat_y = until_params.enter_context(nc.sbuf_tensor("stat_y", [C, LAST * STAT], F32))
        with ExitStack() as ph:
            xs = ph.enter_context(nc.sbuf_tensor("xs1", [C, 2, STRIP], F32))
            ys = ph.enter_context(nc.sbuf_tensor("ys", [C, 2, STRIP], F32))

            def ps_(name, shape):
                return ph.enter_context(nc.psum_tensor(name, shape, F32))

            def sem_(name):
                return ph.enter_context(nc.semaphore(name))

            def sb_(name, shape):
                return ph.enter_context(nc.sbuf_tensor(name, shape, F32))

            QR = C + NH
            wqkv_sb = sb_("wqkv_sb", [C, 3 * C])
            wqkv_hi, wqkv_lo = (ph.enter_context(nc.sbuf_tensor(n, [C, 3 * C], F32R)) for n in ("wqkv_hi", "wqkv_lo"))
            xn_hi, xn_lo = (ph.enter_context(nc.sbuf_tensor(n, [C, 2, TOK], F32R)) for n in ("xn_hi", "xn_lo"))
            wp_sb = sb_("wp_sb", [C, C])
            head96_sb = sb_("head96_sb", [QR, C])
            head8_sb = sb_("head8_sb", [QR, NH])
            keps_sb = sb_("keps_sb", [QR, 1])
            xn = sb_("xn", [C, PAIRS, TOK])
            q_sb = sb_("q_sb", [QR, 2, TOK])
            qsq = sb_("qsq", [C, TOK])
            ksq = sb_("ksq", [128, TG * C])
            knorm = sb_("knorm", [128, 3, TG * NH])
            khat = sb_("khat", [128, TG, QR])
            v_sb = sb_("v_sb", [128, TG, C + 1])
            kv_sb = sb_("kv_sb", [QR, 2, QR])
            den_sb = sb_("den_sb", [QR, TOK])
            rden = sb_("rden", [128, TG * NH])
            rden_x = sb_("rden_x", [128, TG, C])
            rb_sb = sb_("rb_sb", [C, TOK])
            att = sb_("att", [C, TOK])
            yt = sb_("yt", [C, 2, TOK])
            junk = sb_("junk", [C, TOK])
            cxy8 = sb_("cxy8", [C, 2, PAIRS])

            ps_q = ps_("ps_q", [C, TOK])
            ps_kv = ps_("ps_kv", [128, TG, 256])
            ps_g = ps_("ps_g", [128, 512])
            ps_nums = [ps_(f"ps_num{k}", [QR, TOK]) for k in range(2)]
            ps_rb = ps_("ps_rb", [128, TOK])
            ps_qn = ps_("ps_qn", [128, TOK])
            ps_y = ps_qn[0:C, :]
            GW = C + 1
            den_at = ps_rb[:, 0:TG * NH]

            w_in = sem_("w_in")
            w_hi, w_split = sem_("w_hi"), sem_("w_split")
            xhi_ready, xlo_ready = sem_("xhi_ready"), sem_("xlo_ready")
            den_copied, rb_ready = sem_("den_copied"), sem_("rb_ready")
            ones_set = sem_("ones_set")
            x_in = [sem_(f"xb_in{k}") for k in range(2)]
            y_stored = [sem_(f"y_stored{k}") for k in range(2)]
            xn_ready = sem_("xn_ready")
            q_ready, kv_ready = sem_("q_ready"), sem_("kv_ready")
            q_copied, qsq_ready, ksq_ready, v_copied = (sem_(n) for n in ("q_copied", "qsq_ready", "ksq_ready", "v_copied"))
            kss_ready, kn_ready, krec_ready, khat_ready = (sem_(n) for n in ("kss_ready", "kn_ready", "krec_ready", "khat_ready"))
            qss_ready, qn_ready = sem_("qss_ready"), sem_("qn_ready")
            g_ready, gm_ready = sem_("g_ready"), sem_("gm_ready")
            den_ready, rden_ready, rdenx_ready = sem_("den_ready"), sem_("rden_ready"), sem_("rdenx_ready")
            num_ready, rb_copied, att_ready = sem_("num_ready"), sem_("rb_copied"), sem_("att_ready")
            y_ready, y_copied, y_counted, xy_counted = (sem_(n) for n in ("y_ready", "y_copied", "y_counted", "xy_counted"))
            xy_summed = sem_("xy_summed")
            y_placed, pool_turn, pe_turn, act_turn = (sem_(n) for n in ("y_placed", "pool_turn", "pe_turn", "act_turn"))
            block = ph.enter_context(nc.Block())

            @block.sync
            def _(sp):
                for dst, src in ((wqkv_sb, wqkv_t), (wp_sb, wp_t), (head96_sb, head96), (head8_sb, head8),
                                 (keps_sb, keps)):
                    sp.dma_start(dst[:], src).then_inc(w_in, 16)

                def load(n, k):
                    b, s = (n // STRIPS_IMG, n % STRIPS_IMG)
                    sp.dma_start(xs[:, k, :], x_strips[bass.ds(b, 1), bass.ds(s, 1)].squeeze()).then_inc(x_in[k], 16)

                def store(n, k):
                    b, s = (n // STRIPS_IMG, n % STRIPS_IMG)
                    sp.dma_start(y_strips[bass.ds(b, 1), bass.ds(s, 1)].squeeze(), ys[:, k, :]).then_inc(y_stored[k], 16)

                for k in range(2):
                    load(k, k)
                with sp.Fori(0, STRIPS // 2 - 1) as m:
                    for k in range(2):
                        sp.wait_ge(xn_ready, (m * 2 + k + 1) * PAIRS)
                        load(m * 2 + (k + 2), k)
                        sp.wait_ge(y_placed, (m * 2 + k + 1) * PAIRS)
                        store(m * 2 + k, k)
                for n in (STRIPS - 2, STRIPS - 1):
                    sp.wait_ge(y_placed, (n + 1) * PAIRS)
                    store(n, n % 2)
                for k in range(2):
                    sp.wait_ge(y_stored[k], 16 * STRIPS // 2)

            @block.scalar
            def _(act):
                s_ = nc.scalar

                def normalise(n, k, j):
                    u = n * PAIRS + j
                    b = n // STRIPS_IMG
                    src = xs[:, k, :].rearrange("p (r g c) -> p g r c", r=WS, c=WS)[:, 2 * j:2 * j + 2]
                    dst = xn[:, j, :].rearrange("p (g r c) -> p g r c", g=2, r=WS)
                    s_.activation(dst, src, ACT.Identity, scale=r0[:, bass.ds(b, 1)], bias=nb0[:, bass.ds(b, 1)]
                                  ).then_inc(xn_ready, 1)

                def copy_y(n, j, first=False):
                    u = n * PAIRS + j
                    if not first:
                        act.wait_ge(xy_counted, u - 1)
                        act.wait_ge(y_placed, u - 1)
                    act.wait_ge(y_ready, u + 1)
                    s_.activation(yt[:, j % 2, :], ps_y, ACT.Copy).then_inc(y_copied, 1)

                def back(n, k, j, d):
                    return (n, k, j - d) if j >= d else (n - 1, 1 - k, j - d + PAIRS)

                def step(n, k, j, first=False, last=False, load_no=None):
                    u = n * PAIRS + j
                    if not (first and j < 2):
                        copy_rb(u - 2)
                    act.wait_ge(kv_ready, u + 1)
                    s_.activation(ksq[:].rearrange("p (g c) -> p g c", g=TG), ps_kv[:, :, 0:C], ACT.Square
                                  ).then_inc(ksq_ready, 1)
                    s_.activation(v_sb[:, :, 0:C], ps_kv[:, :, C:2 * C], ACT.Copy).then_inc(v_copied, 1)
                    if not (first and j < 1):
                        copy_den(u - 1, (j - 1) % 2)
                    act.wait_ge(kss_ready, u + 1)
                    s_.activation(knorm[:, 1, :], knorm[:, 0, :], ACT.Sqrt).then_inc(kn_ready, 1)
                    act.wait_ge(q_ready, u + 1)
                    s_.activation(q_sb[0:C, j % 2, :], ps_q[:], ACT.Copy).then_inc(q_copied, 1)
                    s_.activation(qsq[:], ps_q[:], ACT.Square).then_inc(qsq_ready, 1)
                    if not (first and j < 2):
                        nn, _, jj = back(n, k, j, 2)
                        copy_y(nn, jj, first and j < 4)
                    if not (first and j < 1):
                        spread(u - 1)
                    if j + 3 == PAIRS and not last:
                        act.wait_ge(x_in[1 - k], load_no)
                    act.wait_ge(qss_ready, u + 1)
                    s_.activation(q_sb[C:QR, j % 2, :], ps_qn[C:QR, :], ACT.Sqrt).then_inc(qn_ready, 1)
                    if j + 3 < PAIRS:
                        normalise(n, k, j + 3)
                    elif not last:
                        normalise(n + 1, 1 - k, j + 3 - PAIRS)

                def copy_den(u, slot):
                    act.wait_ge(num_ready, u + 1)
                    s_.activation(den_sb[C:QR, :], ps_nums[slot][C:QR, :], ACT.Copy).then_inc(den_copied, 1)

                def spread(u):
                    act.wait_ge(rden_ready, u + 1)
                    s_.activation(rden_x[:].rearrange("p g (h c) -> p (g h) c", h=NH),
                                  rden[:].unsqueeze(2).to_broadcast([128, TG * NH, HD]), ACT.Copy
                                  ).then_inc(rdenx_ready, 1)

                def copy_rb(u):
                    act.wait_ge(rb_ready, u + 1)
                    s_.activation(rb_sb[:], ps_rb[0:C, :], ACT.Copy).then_inc(rb_copied, 1)

                act.wait_ge(w_in, 80)
                s_.activation(wqkv_hi[:], wqkv_sb[:], ACT.Copy).then_inc(w_hi, 1)
                act.wait_ge(x_in[0], 16)
                for j in range(3):
                    normalise(0, 0, j)
                for k in range(2):
                    for j in range(PAIRS):
                        step(k, k, j, first=k == 0, load_no=16 * (k + 1))
                with act.Fori(1, STRIPS // 2 - 1) as m:
                    for k in range(2):
                        for j in range(PAIRS):
                            step(m * 2 + k, k, j, load_no=(m + 1 + k) * 16)
                m = STRIPS // 2 - 1
                for k in range(2):
                    for j in range(PAIRS):
                        step(2 * m + k, k, j, last=k == 1, load_no=16 * (m + 1 + k))
                copy_rb(LAST - 2)
                copy_den(LAST - 1, 1)
                copy_y(STRIPS - 1, PAIRS - 2)
                spread(LAST - 1)
                copy_rb(LAST - 1)
                copy_y(STRIPS - 1, PAIRS - 1)

            @block.gpsimd
            def _(pool):
                nc.gpsimd.memset(khat[:, :, C:QR], 1.0).then_inc(ones_set, 1)
                nc.gpsimd.memset(v_sb[:, :, C:C + 1], 1.0).then_inc(ones_set, 1)

                def leading(u, j, first=False):
                    pool.wait_ge(xn_ready, u + 1)
                    if not first:
                        pool.wait_ge(q_ready, u - 1)
                    pool.sem_inc(pool_turn, 1)
                    nc.gpsimd.tensor_copy(xn_hi[:, j % 2, :], xn[:, j, :]).then_inc(xhi_ready, 1)

                def place(n, k, j, stored_no=None):
                    if j == 0 and stored_no is not None:
                        pool.wait_ge(y_stored[k], stored_no)
                    pool.wait_ge(y_copied, n * PAIRS + j + 1)
                    pool.sem_inc(pool_turn, 1)
                    dst = ys[:, k, :].rearrange("p (r g c) -> p g r c", r=WS, c=WS)[:, 2 * j:2 * j + 2]
                    nc.gpsimd.tensor_copy(dst, yt[:, j % 2, :].rearrange("p (g r c) -> p g r c", g=2, r=WS)
                                          ).then_inc(y_placed, 1)

                def strips(m, first=False, last=False):
                    for k in range(2):
                        for j in range(PAIRS):
                            n = m * 2 + k
                            if not (last and k == 1 and j >= PAIRS - 2):
                                leading(n * PAIRS + (j + 2), (j + 2) % PAIRS)
                            if j >= 2:
                                place(n, k, j - 2, None if first else m * 16)
                            elif not (first and k == 0):
                                place(n - 1, 1 - k, j - 2 + PAIRS)

                leading(0, 0, True)
                leading(1, 1, True)
                strips(0, first=True)
                with pool.Fori(1, STRIPS // 2 - 1) as m:
                    strips(m)
                strips(STRIPS // 2 - 1, last=True)
                for j in (PAIRS - 2, PAIRS - 1):
                    place(STRIPS - 1, 1, j)

            @block.tensor
            def _(pe):
                mm = nc.tensor.matmul

                def split(out_, w, xx, last=False):
                    (w_hi_, w_lo_), (x_hi_, x_lo_) = w, xx
                    mm(out_, w_hi_, x_hi_, start=True, stop=False)
                    mm(out_, w_hi_, x_lo_, start=False, stop=False)
                    return mm(out_, w_lo_, x_hi_, start=False, stop=True)

                def project_q(u, j, first):
                    if not first:
                        pe.wait_ge(q_copied, u)
                    split(ps_q[:], (wqkv_hi[:, 0:C], wqkv_lo[:, 0:C]), (xn_hi[:, j % 2, :], xn_lo[:, j % 2, :])
                          ).then_inc(q_ready, 1)

                def project_kv(u, j, back):
                    pe.wait_ge(xlo_ready, u + 1)
                    for g in range(TG):
                        at = slice(g * 128, (g + 1) * 128)
                        last = split(ps_kv[:, g, 0:2 * C], (xn_hi[:, j % 2, at], xn_lo[:, j % 2, at]),
                                     (wqkv_hi[:, C:3 * C], wqkv_lo[:, C:3 * C]))
                        if g == 0 and back:
                            turn_back(u - 2)
                    last.then_inc(kv_ready, 1)

                def numerators(u, j):
                    pe.wait_ge(qn_ready, u + 1)
                    pe.wait_ge(gm_ready, u + 1)
                    for w in range(2):
                        last = mm(ps_nums[j % 2][:, w * WIN:(w + 1) * WIN], kv_sb[:, w, :], q_sb[:, j % 2, w * WIN:(w + 1) * WIN],
                                  start=True, stop=True)
                    last.then_inc(num_ready, 1)

                def turn_den(u):
                    pe.wait_ge(den_copied, u + 1)
                    pe.sem_inc(pe_turn, 1)
                    for g in range(TG):
                        last = nc.tensor.transpose(den_at[:, g * NH:(g + 1) * NH], den_sb[C:QR, g * 128:(g + 1) * 128],
                                                   ident_sb[C:QR, C:QR])
                    last.then_inc(den_ready, 1)

                def turn_back(u):
                    pe.wait_ge(rdenx_ready, u + 1)
                    for g in range(TG):
                        last = nc.tensor.transpose(ps_rb[0:C, g * 128:(g + 1) * 128], rden_x[:, g, :], ident_sb[:])
                    last.then_inc(rb_ready, 1)

                def q_norms(u):
                    pe.wait_ge(qsq_ready, u + 1)
                    mm(ps_qn[C:QR, :], head8_sb[0:C, :], qsq[:], start=True, stop=True).then_inc(qss_ready, 1)

                def kv_sums(u):
                    pe.wait_ge(khat_ready, u + 1)
                    pe.wait_ge(v_copied, u + 1)
                    for g in range(TG):
                        w = g // 2
                        last = mm(ps_g[0:QR, w * GW:(w + 1) * GW], khat[:, g, :], v_sb[:, g, :], start=g % 2 == 0,
                                  stop=g % 2 == 1)
                    last.then_inc(g_ready, 1)

                def project_y(u, first):
                    pe.wait_ge(att_ready, u + 1)
                    if not first:
                        pe.wait_ge(y_copied, u)
                    mm(ps_y, wp_sb[:], att[:], start=True, stop=True).then_inc(y_ready, 1)

                def step(u, j, first=False):
                    one, two = not (first and j < 1), not (first and j < 2)
                    project_kv(u, j, two)
                    if one:
                        numerators(u - 1, j - 1)
                    project_q(u, j, not one)
                    if two:
                        project_y(u - 2, first and j == 2)
                    if one:
                        turn_den(u - 1)
                    q_norms(u)
                    kv_sums(u)

                pe.wait_ge(w_in, 80)
                pe.wait_ge(w_split, 1)
                pe.wait_ge(ones_set, 2)
                for j in range(PAIRS):
                    step(j, j, first=True)
                with pe.Fori(1, STRIPS) as n:
                    for j in range(PAIRS):
                        step(n * PAIRS + j, j)
                turn_back(LAST - 2)
                numerators(LAST - 1, PAIRS - 1)
                project_y(LAST - 2, False)
                turn_den(LAST - 1)
                turn_back(LAST - 1)
                project_y(LAST - 1, False)

            @block.vector
            def _(dve):
                v = nc.vector

                def invert_den(u):
                    dve.wait_ge(den_ready, u + 1)
                    v.reciprocal(rden[:], den_at).then_inc(rden_ready, 1)

                def square_sums(u):
                    dve.wait_ge(ksq_ready, u + 1)
                    v.tensor_reduce(knorm[:, 0, :], ksq[:].rearrange("p (h c) -> p h c", c=HD), AX.X, ALU.add
                                    ).then_inc(kss_ready, 1)

                def unit_k(u):
                    dve.wait_ge(kn_ready, u + 1)
                    v.reciprocal(knorm[:, 2, :], knorm[:, 1, :]).then_inc(krec_ready, 1)
                    dve.wait_ge(krec_ready, u + 1)
                    v.tensor_tensor(khat[:, :, 0:C].rearrange("p g (h c) -> p g h c", c=HD),
                                    ps_kv[:, :, 0:C].rearrange("p g (h c) -> p g h c", c=HD),
                                    knorm[:, 2, :].rearrange("p (g h) -> p g h", g=TG).unsqueeze(3).to_broadcast(
                                        [128, TG, NH, HD]), ALU.mult).then_inc(khat_ready, 1)

                def attend(u, slot):
                    dve.wait_ge(rb_copied, u + 1)
                    v.tensor_tensor(att[:], ps_nums[slot][0:C, :], rb_sb[:], ALU.mult).then_inc(att_ready, 1)

                def window_sums(u):
                    dve.wait_ge(g_ready, u + 1)
                    g = ps_g[0:QR, 0:2 * GW].rearrange("p (w c) -> p w c", w=2)
                    v.tensor_tensor(kv_sb[:, :, 0:C], g[:, :, 0:C], head96_sb[:].unsqueeze(1).to_broadcast([QR, 2, C]), ALU.mult)
                    for w in range(2):
                        last = v.scalar_tensor_tensor(out=kv_sb[:, w, C:QR], in0=g[:, w, C:C + 1].to_broadcast([QR, NH]),
                                                      scalar=keps_sb[:], in1=head8_sb[:], op0=ALU.add, op1=ALU.mult)
                    last.then_inc(gm_ready, 1)

                def count_y(u, j):
                    dve.wait_ge(y_copied, u + 1)
                    v.bn_stats(stat_y[:, bass.ds(u * STAT, STAT)], yt[:, j % 2, :]).then_inc(y_counted, 1)

                def count_xy(u, j):
                    v.tensor_tensor_reduce(out=junk[:], in0=yt[:, j % 2, :], in1=xn[:, j, :], scale=1.0, scalar=0.0,
                                           op0=ALU.mult, op1=ALU.add, accum_out=cxy8[:, 0, j:j + 1]
                                           ).then_inc(xy_counted, 1)

                def sum_strip(n):
                    dve.wait_ge(xy_counted, (n + 1) * PAIRS)
                    v.tensor_reduce(cxy_strip[:, bass.ds(n, 1)], cxy8[:, 0, :], AX.X, ALU.add).then_inc(xy_summed, 1)

                def trailing(u, j):
                    dve.wait_ge(xhi_ready, u + 1)
                    v.tensor_tensor(xn_lo[:, j % 2, :], xn[:, j, :], xn_hi[:, j % 2, :].bitcast(F32), ALU.subtract
                                    ).then_inc(xlo_ready, 1)

                def step(u, j, n, first=False, last=False):
                    if not (first and j < 2):
                        attend(u - 2, j % 2)
                    square_sums(u)
                    if not (first and j < 3):
                        count_xy(u - 3, (j - 3) % PAIRS)
                    unit_k(u)
                    if j == 2 and not first:
                        sum_strip(n - 1)
                    if not (first and j < 1):
                        invert_den(u - 1)
                    if not (last and j >= PAIRS - 2):
                        trailing(u + 2, (j + 2) % PAIRS)
                    if j == 2 and not first:
                        dve.wait_ge(xy_summed, n)
                    window_sums(u)
                    if not (first and j < 2):
                        count_y(u - 2, (j - 2) % PAIRS)

                dve.wait_ge(w_in, 80)
                dve.wait_ge(w_hi, 1)
                v.tensor_tensor(wqkv_lo[:], wqkv_sb[:], wqkv_hi[:].bitcast(F32), ALU.subtract).then_inc(w_split, 1)
                trailing(0, 0)
                trailing(1, 1)
                for j in range(PAIRS):
                    step(j, j, 0, first=True)
                with dve.Fori(1, STRIPS - 1) as n:
                    for j in range(PAIRS):
                        step(n * PAIRS + j, j, n)
                for j in range(PAIRS):
                    step(LAST - PAIRS + j, j, STRIPS - 1, last=True)
                attend(LAST - 2, 0)
                invert_den(LAST - 1)
                count_xy(LAST - 3, PAIRS - 3)
                count_y(LAST - 2, PAIRS - 2)
                dve.wait_ge(xy_counted, LAST - 2)
                count_xy(LAST - 2, PAIRS - 2)
                attend(LAST - 1, 1)
                count_y(LAST - 1, PAIRS - 1)
                dve.wait_ge(xy_counted, LAST - 1)
                count_xy(LAST - 1, PAIRS - 1)
                sum_strip(STRIPS - 1)
                dve.wait_ge(xy_summed, STRIPS)
                dve.wait_ge(y_counted, LAST)

        with ExitStack() as ph:
            def sb_(name, shape):
                return ph.enter_context(nc.sbuf_tensor(name, shape, F32))

            def sem_(name):
                return ph.enter_context(nc.semaphore(name))

            mv = sb_("mv2", [C, B, 2])
            mean_y, var_y, cxy, mean_n = (sb_(n, [C, B]) for n in ("mean_y", "var_y", "cxy", "mean_n"))
            tmp, m1, v1, r1 = (sb_(n, [C, B]) for n in ("tmp", "m1", "v1", "r1"))
            s1 = sb_("s1", [C, 8])
            par = sb_("par", [C, NPAR])
            ps_m = ph.enter_context(nc.psum_tensor("ps_m2", [C, 512], F32))
            ps_v = ph.enter_context(nc.psum_tensor("ps_v2", [C, 512], F32))
            veps, sd, means, gmeans, vars_, gvars, par_set, par_out, chain = (
                sem_(n) for n in ("veps2", "sd2", "means2", "gmeans2", "vars2", "gvars2", "par_set", "par_out", "chain2"))
            block = ph.enter_context(nc.Block())

            @block.scalar
            def _(act):
                act.wait_ge(veps, 1)
                nc.scalar.activation(s1[:, 2:3], s1[:, 1:2], ACT.Sqrt).then_inc(sd, 1)
                act.wait_ge(veps, 2)
                nc.scalar.activation(tmp[:], v1[:], ACT.Sqrt).then_inc(sd, 1)

            @block.tensor
            def _(pe):
                pe.wait_ge(means, 1)
                nc.tensor.matmul(ps_m[:, 0:B], gmean_sb[:], m1[:], start=True, stop=True).then_inc(gmeans, 1)
                pe.wait_ge(vars_, 1)
                nc.tensor.matmul(ps_v[:, 0:B], gmean_sb[:], v1[:], start=True, stop=True).then_inc(gvars, 1)

            @block.sync
            def _(sp):
                sp.wait_ge(par_set, 1)
                sp.dma_start(par_dram, par[:]).then_inc(par_out, 16)
                sp.wait_ge(par_out, 16)

            @block.vector
            def _(dve):
                v = nc.vector
                steps = [0]

                def link(ins):
                    steps[0] += 1
                    ins.then_inc(chain, 1)
                    dve.wait_ge(chain, steps[0])

                def tt(o, a, b, op):
                    link(v.tensor_tensor(o, a, b, op))

                n_img = float(H * W)
                for b in range(B):
                    last = v.bn_aggr(mv[:, b, :], stat_y[:, b * 128 * STAT:(b + 1) * 128 * STAT])
                link(last)
                v.tensor_copy(mean_y[:], mv[:, :, 0])
                link(v.tensor_copy(var_y[:], mv[:, :, 1]))
                link(v.tensor_reduce(s1[:, 0:1], mean_y[:], AX.X, ALU.add))
                link(v.tensor_scalar(s1[:, 0:1], s1[:, 0:1], 1.0 / B, None, ALU.mult))
                link(v.tensor_scalar(tmp[:], mean_y[:], s1[:, 0:1], None, ALU.subtract))
                tt(tmp[:], tmp[:], tmp[:], ALU.mult)
                tt(tmp[:], tmp[:], var_y[:], ALU.add)
                link(v.tensor_reduce(s1[:, 1:2], tmp[:], AX.X, ALU.add))
                link(v.tensor_scalar(s1[:, 1:2], s1[:, 1:2], 1.0 / B, BN_EPS, ALU.mult, ALU.add))
                dve.sem_inc(veps, 1)
                dve.wait_ge(sd, 1)
                link(v.reciprocal(s1[:, 3:4], s1[:, 2:3]))
                tt(s1[:, 4:5], s1[:, 3:4], gb[:, 0:1], ALU.mult)
                tt(s1[:, 5:6], s1[:, 0:1], s1[:, 4:5], ALU.mult)
                tt(s1[:, 5:6], gb[:, 1:2], s1[:, 5:6], ALU.subtract)
                link(v.tensor_reduce(cxy[:], cxy_strip[:].rearrange("p (b s) -> p b s", b=B), AX.X, ALU.add))
                tt(mean_n[:], mean_x[:], gm0[:], ALU.subtract)
                tt(mean_n[:], mean_n[:], r0[:], ALU.mult)
                tt(mean_n[:], mean_n[:], mean_y[:], ALU.mult)
                link(v.scalar_tensor_tensor(out=cxy[:], in0=cxy[:], scalar=1.0 / n_img, in1=mean_n[:], op0=ALU.mult,
                                            op1=ALU.subtract))
                link(v.reciprocal(tmp[:], r0[:]))
                tt(cxy[:], cxy[:], tmp[:], ALU.mult)
                link(v.scalar_tensor_tensor(out=m1[:], in0=mean_y[:], scalar=s1[:, 4:5], in1=mean_x[:], op0=ALU.mult,
                                            op1=ALU.add))
                link(v.tensor_scalar(m1[:], m1[:], s1[:, 5:6], None, ALU.add))
                dve.sem_inc(means, 1)
                link(v.tensor_scalar(tmp[:], var_y[:], s1[:, 4:5], None, ALU.mult))
                link(v.scalar_tensor_tensor(out=tmp[:], in0=cxy[:], scalar=2.0, in1=tmp[:], op0=ALU.mult, op1=ALU.add))
                link(v.scalar_tensor_tensor(out=v1[:], in0=tmp[:], scalar=s1[:, 4:5], in1=var_x[:], op0=ALU.mult,
                                            op1=ALU.add))
                dve.wait_ge(gmeans, 1)
                tt(tmp[:], m1[:], ps_m[:, 0:B], ALU.subtract)
                link(v.tensor_copy(m1[:], ps_m[:, 0:B]))
                tt(tmp[:], tmp[:], tmp[:], ALU.mult)
                tt(v1[:], v1[:], tmp[:], ALU.add)
                dve.sem_inc(vars_, 1)
                dve.wait_ge(gvars, 1)
                link(v.tensor_scalar(v1[:], ps_v[:, 0:B], GN_EPS, None, ALU.add))
                dve.sem_inc(veps, 1)
                dve.wait_ge(sd, 2)
                link(v.reciprocal(r1[:], tmp[:]))
                link(v.tensor_scalar(tmp[:], m1[:], s1[:, 5:6], -1.0, ALU.subtract, ALU.mult))
                tt(par[:, 2 + B:2 + 2 * B], tmp[:], r1[:], ALU.mult)
                link(v.tensor_copy(par[:, 2:2 + B], r1[:]))
                link(v.tensor_copy(par[:, 0:1], s1[:, 4:5]))
                tt(par[:, 1:2], s1[:, 5:6], gb[:, 2:3], ALU.add)
                dve.sem_inc(par_set, 1)

        until_params.close()

        with ExitStack() as ph:
            def ps_(name, shape):
                return ph.enter_context(nc.psum_tensor(name, shape, F32))

            def sem_(name):
                return ph.enter_context(nc.semaphore(name))

            def sb_(name, shape):
                return ph.enter_context(nc.sbuf_tensor(name, shape, F32))

            def sbr_(name, shape):
                return ph.enter_context(nc.sbuf_tensor(name, shape, F32R))

            LO, HI = 1, 0
            x1 = [sb_(f"x1_{g}", [128, PAIRW, IMGS, W]) for g in range(SETS)]
            xb = sb_("xb", [128, PAIRW, IMGS, W])
            yb = sb_("yb", [128, PAIRW, IMGS, W])
            ob = sb_("ob", [128, PAIRW, IMGS, W])
            z = sb_("z", [128, WINDOWS, IMGS, HALF])
            zb = [[sbr_(f"zb{g}_{h}", [128, WINDOWS, IMGS, ZW]) for h in range(2)] for g in range(SETS)]
            raw1 = sb_("raw1", [128, 2 * TAPS, WROWS])
            raw2 = sb_("raw2", [128, 2 * TAPS, HALF])
            raw3 = sb_("raw3", [128, 2 * TAPS, HALF])
            mat1 = [[sbr_(f"mat1_{k}_{h}", [128, TAPS, 2 * WROWS]) for h in range(2)] for k in range(2)]
            mat2 = [[sbr_(f"mat2_{k}_{h}", [128, 2, TAPS, HALF]) for h in range(2)] for k in range(2)]
            mat3 = [[sbr_(f"mat3_{k}_{h}", [128, 2, TAPS, HALF]) for h in range(2)] for k in range(2)]
            prm = [sb_(f"prm_{k}", [128, NPAR]) for k in range(2)]
            shift = [sb_(f"shift_{k}", [128, PAIRW, B]) for k in range(2)]
            down_sb = sbr_("down_sb", [128, WINDOWS, HALF])
            up_sb = sbr_("up_sb", [128, WINDOWS, 2 * WROWS])
            inside_sb = sb_("inside_sb", [128, PAIRW])
            ll1 = sb_("ll1", [128, IMGS, HALF])
            in2 = sb_("in2", [128, 2, IMGS, HALF // 2])
            in3 = sb_("in3", [128, 2, IMGS, HALF // 4])
            in2_p = [sbr_(f"in2_{h}", [128, 2, IMGS, HALF // 2 + 4]) for h in range(2)]
            in3_p = [sbr_(f"in3_{h}", [128, 2, IMGS, HALF // 4 + 4]) for h in range(2)]
            next_p = [sbr_(f"next_{h}", [128, IMGS * HALF]) for h in range(2)]
            s3 = sb_("s3", [128, IMGS * HALF // 4])
            up3 = sb_("up3", [128, IMGS * HALF // 4, 2])
            low2 = sb_("low2", [128, IMGS * HALF // 2])
            next_ll = sb_("next_ll", [128, IMGS * HALF // 2, 2])
            ps_w = [ps_(f"ps_w{t}", [128, IMGS * HALF]) for t in range(WINDOWS)]
            ps_ll = ps_("ps_ll", [128, IMGS * HALF])
            ps_2 = ps_("ps_2", [128, 2, IMGS * HALF // 2])
            ps_3 = ps_("ps_3", [128, 2, 256])

            prm_in = [sem_(f"prm_in{k}") for k in range(2)]
            pool_turn, sp_turn = sem_("pool_turn_c"), sem_("sp_turn")
            raw_in, mats_hi, mats_ready = sem_("raw_in"), sem_("mats_hi"), sem_("mats_ready")
            const_in, zeroed = sem_("constc_in"), sem_("zeroed")
            xy_in, down_set = sem_("xy_in"), sem_("down_set")
            z_hi, z_lo, in2_hi, in2_lo, in3_hi, in3_lo, next_hi, next_lo = (
                sem_(n) for n in ("z_hi", "z_lo", "in2_hi", "in2_lo", "in3_hi", "in3_lo", "next_hi", "next_lo"))
            x1_ready, shift_ready, z_act, z_dve = (sem_(n) for n in ("x1_ready", "shift_ready", "z_act", "z_dve"))
            ll_ready, ll_copied, in2_ready, in3_ready = (sem_(n) for n in ("ll_ready", "ll_copied", "in2_ready", "in3_ready"))
            l3_ready, s3_copied, up3_ready, l2_ready, low2_ready, next_ready = (
                sem_(n) for n in ("l3_ready", "s3_copied", "up3_ready", "l2_ready", "low2_ready", "next_ready"))
            win_ready = sem_("win_ready")
            out_ready = sem_("out_ready")
            LEAD = 3 * WINDOWS
            stored = sem_("stored")
            block = ph.enter_context(nc.Block())
            NLOAD = 2 * WINDOWS * 16
            NRAW = (4 + 2 + 4) * 16

            def zero_pads(eng):
                for t_ in (xb, yb, *zb[0], *zb[1], *in2_p, *in3_p):
                    eng.memset(t_[:].bitcast(F32), 0.0).then_inc(zeroed, 1)

            N_ZERO = 2 + 2 * SETS + 4

            down_raw = z[:, 0:2].rearrange("p t b w -> p (t b w)")[:, 0:WINDOWS * HALF].rearrange(
                "p (t w) -> p t w", t=WINDOWS)
            up_raw = z[:, 2:4].rearrange("p t b w -> p (t b w)")[:, 0:WINDOWS * HALF].rearrange(
                "p (t w) -> p t w", t=WINDOWS)

            @block.sync
            def _(sp):
                for dst, src in ((down_raw, down), (up_raw, up), (inside_sb[:], inside)):
                    sp.dma_start(dst, src).then_inc(const_in, 16)

                def load_prm(c, k):
                    sp.dma_start(prm[k][:], bass.AP(tensor=par_dram.tensor, offset=c * NPAR, ap=[[0, 128], [1, NPAR]])
                                 ).then_inc(prm_in[k], 16)

                def load_raw(c):
                    for ia in range(2):
                        for q in range(2):
                            first = q * WROWS + ia
                            sp.dma_start(raw1[first:first + WROWS - 1:2, :, :],
                                         bass.AP(tensor=vec1.tensor,
                                                 offset=c * (NV1 * V1) + ((2 * ia + q) * 2 * TAPS * V1 + 2),
                                                 ap=[[2, WROWS // 2], [V1, 2 * TAPS], [1, WROWS]])).then_inc(raw_in, 16)
                    for ia in range(2):
                        sp.dma_start(raw2[ia:128:2, :, :],
                                     bass.AP(tensor=vec2.tensor, offset=c * (NV2 * V2) + (ia * 2 * TAPS * V2 + 2),
                                             ap=[[2, HALF // 2], [V2, 2 * TAPS], [1, HALF]])).then_inc(raw_in, 16)
                    for rho in range(4):
                        sp.dma_start(raw3[rho:128:4, :, :],
                                     bass.AP(tensor=vec3.tensor,
                                             offset=c * (NV2 * V2) + (rho // 2 * 2 * TAPS * V2 + 4),
                                             ap=[[4, HALF // 4], [V2, 2 * TAPS], [1, HALF]])).then_inc(raw_in, 16)

                def load(c, g):
                    for t in range(WINDOWS):
                        lo, hi, skip = window_rows(t)
                        p = (t % 2) * WROWS + skip
                        for dst, src in ((xb, x), (yb, y_dram)):
                            sp.dma_start(dst[p:p + hi - lo, t // 2],
                                         src[IMGS * g:IMGS * (g + 1), bass.ds(c, 1), lo:hi, :].rearrange(
                                             "b o h w -> (o h) b w")).then_inc(xy_in, 16)

                def store(c, g, count):
                    for t in range(WINDOWS):
                        sp.wait_ge(out_ready, count * WINDOWS + (LEAD + t + 1))
                        sp.sem_inc(sp_turn, 1)
                        n = min(OROWS, H - OROWS * t)
                        p = (t % 2) * WROWS + HALO
                        sp.dma_start(out[IMGS * g:IMGS * (g + 1), bass.ds(c, 1), OROWS * t:OROWS * t + n, :].rearrange(
                            "b o h w -> (o h) b w"), ob[p:p + n, t // 2]).then_inc(stored, 16)

                def group(m, k, g, last=False):
                    c = m * 2 + k
                    if not (last and k == 1):
                        sp.wait_ge(x1_ready, m * (4 * PAIRW) + (2 * k + g + 2) * PAIRW)
                        sp.sem_inc(sp_turn, 1)
                        load(c + 1, g)
                    store(c, g, m * 4 + (2 * k + g))

                sp.wait_ge(zeroed, N_ZERO)
                load_raw(0)
                sp.sem_inc(stored, 16)
                for k in range(2):
                    load_prm(k, k)
                load(0, 0)
                sp.wait_ge(x1_ready, PAIRW)
                load(0, 1)
                sp.wait_ge(mats_ready, 1)
                load_raw(1)
                with sp.Fori(0, C // 2 - 1) as m:
                    for k in range(2):
                        for g in range(SETS):
                            group(m, k, g)
                            if g == 0:
                                sp.wait_ge(mats_ready, m * 2 + (k + 2))
                                load_raw(m * 2 + (k + 2))
                        load_prm(m * 2 + (k + 2), k)
                for k in range(2):
                    for g in range(SETS):
                        group(C // 2 - 1, k, g, last=True)
                sp.wait_ge(stored, 16 * WINDOWS * C * SETS + 16)

            @block.gpsimd
            def _(pool):
                zero_pads(nc.gpsimd)
                with pool.Fori(0, C // 2) as m:
                    for k in range(2):
                        pool.wait_ge(raw_in, m * (2 * NRAW) + (k + 1) * NRAW)
                        pool.wait_ge(out_ready, m * (4 * WINDOWS) + (2 * k - 2) * WINDOWS + LEAD)
                        pool.sem_inc(pool_turn, 1)
                        turned = ((mat1[k], raw1[:].rearrange("p (d o) m -> p d (o m)", o=2)[:, :, ::-1], "p d m -> p d m"),
                                  (mat2[k], raw2[:, :, ::-1], "p s d m -> p (s d) m"),
                                  (mat3[k], raw3[:, :, ::-1], "p s d m -> p (s d) m"))
                        for mat, raw, form in turned:
                            last = nc.gpsimd.tensor_copy(mat[HI][:].rearrange(form), raw)
                        last.then_inc(mats_hi, 1)
                        pool.wait_ge(mats_hi, m * 2 + (k + 1))
                        pool.sem_inc(pool_turn, 1)
                        for mat, raw, form in turned:
                            last = nc.gpsimd.tensor_tensor(mat[LO][:].rearrange(form), raw,
                                                           mat[HI][:].bitcast(F32).rearrange(form), ALU.subtract)
                        last.then_inc(mats_ready, 1)

            def z_ops(eng_op, k, g, t, q):
                p = (t % 2) * WROWS
                for b in range(IMGS):
                    img = IMGS * g + b
                    last = eng_op(z[q * WROWS:(q + 1) * WROWS, t, b, :],
                                  x1[g][p:p + WROWS, t // 2, b, q::2],
                                  prm[k][p:p + WROWS, 2 + img:3 + img], shift[k][p:p + WROWS, t // 2, img:img + 1])
                return last

            DVE_T = range(3)
            ACT_T = range(3, WINDOWS)
            N_ACT = WINDOWS + len(ACT_T)

            def next_group(m, k, g):
                return (m, k, 1) if g == 0 else (m, 1, 0) if k == 0 else (m + 1, 0, 0)

            def groups(steps):
                def pair(m, end=False):
                    for k in range(2):
                        for g in range(SETS):
                            steps(m, k, g, end and (k, g) == (1, 1))
                return pair

            @block.scalar
            def _(act):
                def norm(o, i, scale, bias):
                    return nc.scalar.activation(o, i, ACT.Identity, scale=scale, bias=bias)

                def even(m, k, g, ts):
                    act.wait_ge(shift_ready, m * 2 + k + 1)
                    for t in ts:
                        act.wait_ge(x1_ready, m * (4 * PAIRW) + (2 * k + g) * PAIRW + t // 2 + 1)
                        z_ops(norm, k, g, t, 0).then_inc(z_act, 1)

                def odd(k, g):
                    for t in ACT_T:
                        z_ops(norm, k, g, t, 1).then_inc(z_act, 1)

                def leading(qn, g, ts):
                    for t in ts:
                        if t in DVE_T:
                            act.wait_ge(z_dve, qn * len(DVE_T) + t + 1)
                            act.wait_ge(z_act, qn * N_ACT + t + 1)
                        else:
                            act.wait_ge(z_act, qn * N_ACT + (WINDOWS + t - len(DVE_T) + 1))
                        nc.scalar.activation(zb[g][HI][:, t, :, 2:2 + HALF], z[:, t], ACT.Copy).then_inc(z_hi, 1)

                def steps(m, k, g, last):
                    qn = m * 4 + (2 * k + g)
                    m2, k2, g2 = next_group(m, k, g)
                    act.wait_ge(ll_ready, qn + 1)
                    nc.scalar.activation(ll1[:].rearrange("p b w -> p (b w)"), ps_ll[:], ACT.Copy).then_inc(ll_copied, 1)
                    act.wait_ge(in2_ready, qn * 2 + 2)
                    nc.scalar.activation(in2_p[HI][:, :, :, 2:2 + HALF // 2], in2[:], ACT.Copy).then_inc(in2_hi, 1)
                    act.wait_ge(in3_ready, qn + 1)
                    nc.scalar.activation(in3_p[HI][:, :, :, 2:2 + HALF // 4], in3[:], ACT.Copy).then_inc(in3_hi, 1)
                    if not last:
                        even(m2, k2, g2, DVE_T)
                    act.wait_ge(l3_ready, qn + 1)
                    nc.scalar.activation(s3[:], ps_3[:, 0, 0:IMGS * HALF // 4], ACT.Copy).then_inc(s3_copied, 1)
                    if not last:
                        even(m2, k2, g2, ACT_T)
                        odd(k2, g2)
                    act.wait_ge(next_ready, qn + 1)
                    nc.scalar.activation(next_p[HI][:], next_ll[:].rearrange("p n c -> p (n c)"), ACT.Copy
                                         ).then_inc(next_hi, 1)
                    if not last:
                        leading(qn + 1, g2, range(WINDOWS))

                even(0, 0, 0, range(WINDOWS))
                odd(0, 0)
                leading(0, 0, range(WINDOWS))
                pair = groups(steps)
                with act.Fori(0, C // 2 - 1) as m:
                    pair(m)
                pair(C // 2 - 1, True)

            @block.tensor
            def _(pe):
                mm = nc.tensor.matmul

                def split(out_, w, xx, start, stop):
                    mm(out_, w[HI], xx[HI], start=start, stop=False)
                    mm(out_, w[HI], xx[LO], start=False, stop=False)
                    return mm(out_, w[LO], xx[HI], start=False, stop=stop)

                def steps(m, k, g, last_group):
                    qn = m * 4 + (2 * k + g)
                    pe.wait_ge(z_lo, qn * WINDOWS + WINDOWS)
                    for t in range(WINDOWS):
                        for h in (HI, LO):
                            last = mm(ps_ll[:], down_sb[:, t, :], zb[g][h][:, t, :, 2:2 + HALF], start=t + h == 0,
                                      stop=t + h == WINDOWS)
                    last.then_inc(ll_ready, 1)
                    pe.wait_ge(mats_ready, m * 2 + k + 1)

                    def conv(t):
                        pe.wait_ge(out_ready, qn * WINDOWS + (LEAD + t + 1 - WINDOWS))
                        for d in range(TAPS):
                            split(ps_w[t][:], [mat1[k][h][:, d, :] for h in range(2)],
                                  [zb[g][h][:, t, :, d:d + HALF] for h in range(2)], d == 0, False)

                    def level(ps, mat, src, n):
                        for s in range(2):
                            for d in range(TAPS):
                                last = split(ps[:, s, 0:IMGS * n], [mat[k][h][:, s, d, :] for h in range(2)],
                                             [src[h][:, s, :, d:d + n] for h in range(2)], d == 0, d == TAPS - 1)
                        return last

                    for t in range(3):
                        conv(t)
                    pe.wait_ge(in3_lo, qn + 1)
                    level(ps_3, mat3, in3_p, HALF // 4).then_inc(l3_ready, 1)
                    pe.wait_ge(in2_lo, qn + 1)
                    level(ps_2, mat2, in2_p, HALF // 2).then_inc(l2_ready, 1)
                    for t in range(3, WINDOWS):
                        conv(t)
                    pe.wait_ge(next_lo, qn + 1)
                    for t in range(WINDOWS):
                        for h in (HI, LO):
                            last = mm(ps_w[t][:], up_sb[:, t, :], next_p[h][:], start=False, stop=h == LO)
                        last.then_inc(win_ready, 1)

                pe.wait_ge(down_set, 2)
                pe.wait_ge(zeroed, N_ZERO)
                pair = groups(steps)
                with pe.Fori(0, C // 2) as m:
                    pair(m)

            @block.vector
            def _(dve):
                v = nc.vector

                def norm(o, i, scale, bias):
                    return v.tensor_scalar(o, i, scale, bias, ALU.mult, ALU.add)

                def make_x1(m, k, g):
                    qn = m * 4 + (2 * k + g)
                    if g == 0:
                        dve.wait_ge(prm_in[k], m * 16 + 16)
                        v.tensor_tensor(shift[k][:], prm[k][:, 2 + B:2 + 2 * B].unsqueeze(1).to_broadcast([128, PAIRW, B]),
                                        inside_sb[:].unsqueeze(2).to_broadcast([128, PAIRW, B]), ALU.mult
                                        ).then_inc(shift_ready, 1)
                    dve.wait_ge(xy_in, qn * NLOAD + NLOAD)
                    for i in range(PAIRW):
                        n = 128 if 2 * i + 1 < WINDOWS else WROWS
                        v.scalar_tensor_tensor(out=x1[g][0:n, i].rearrange("p b w -> p (b w)"),
                                               in0=yb[0:n, i].rearrange("p b w -> p (b w)"), scalar=prm[k][0:n, 0:1],
                                               in1=xb[0:n, i].rearrange("p b w -> p (b w)"), op0=ALU.mult, op1=ALU.add
                                               ).then_inc(x1_ready, 1)

                def odd(m, k, g):
                    dve.wait_ge(shift_ready, m * 2 + k + 1)
                    dve.wait_ge(x1_ready, m * (4 * PAIRW) + (2 * k + g + 1) * PAIRW)
                    for t in DVE_T:
                        z_ops(norm, k, g, t, 1).then_inc(z_dve, 1)

                def trailing(qn, g, ts):
                    for t in ts:
                        dve.wait_ge(z_hi, qn * WINDOWS + t + 1)
                        v.tensor_tensor(zb[g][LO][:, t, :, 2:2 + HALF], z[:, t],
                                        zb[g][HI][:, t, :, 2:2 + HALF].bitcast(F32), ALU.subtract).then_inc(z_lo, 1)

                def down_levels(qn):
                    dve.wait_ge(ll_copied, qn + 1)
                    for s, op in enumerate((ALU.add, ALU.subtract)):
                        v.tensor_tensor(in2[:, s], ll1[:, :, 0::2], ll1[:, :, 1::2], op).then_inc(in2_ready, 1)
                    dve.wait_ge(in2_ready, qn * 2 + 2)
                    for s, op in enumerate((ALU.add, ALU.subtract)):
                        last = v.tensor_tensor(in3[:, s], in2[:, 0, :, 0::2], in2[:, 0, :, 1::2], op)
                    last.then_inc(in3_ready, 1)
                    for hi, lo, full, part, n in ((in3_hi, in3_lo, in3, in3_p, HALF // 4),
                                                  (in2_hi, in2_lo, in2, in2_p, HALF // 2)):
                        dve.wait_ge(hi, qn + 1)
                        v.tensor_tensor(part[LO][:, :, :, 2:2 + n], full[:], part[HI][:, :, :, 2:2 + n].bitcast(F32),
                                        ALU.subtract).then_inc(lo, 1)

                def up_levels(qn):
                    n = IMGS * HALF // 4
                    dve.wait_ge(s3_copied, qn + 1)
                    v.tensor_tensor(up3[:, :, 0], s3[:], ps_3[:, 1, 0:n], ALU.add)
                    v.tensor_tensor(up3[:, :, 1], s3[:], ps_3[:, 1, 0:n], ALU.subtract).then_inc(up3_ready, 1)
                    dve.wait_ge(l2_ready, qn + 1)
                    dve.wait_ge(up3_ready, qn + 1)
                    v.tensor_tensor(low2[:], up3[:].rearrange("p n c -> p (n c)"), ps_2[:, 0, :], ALU.add
                                    ).then_inc(low2_ready, 1)
                    dve.wait_ge(low2_ready, qn + 1)
                    v.tensor_tensor(next_ll[:, :, 0], low2[:], ps_2[:, 1, :], ALU.add)
                    v.tensor_tensor(next_ll[:, :, 1], low2[:], ps_2[:, 1, :], ALU.subtract).then_inc(next_ready, 1)

                def next_trailing(qn):
                    dve.wait_ge(next_hi, qn + 1)
                    v.tensor_tensor(next_p[LO][:], next_ll[:].rearrange("p n c -> p (n c)"), next_p[HI][:].bitcast(F32),
                                    ALU.subtract).then_inc(next_lo, 1)

                def finish(qn, k, g):
                    for t in range(WINDOWS):
                        p = (t % 2) * WROWS
                        dve.wait_ge(win_ready, qn * WINDOWS + t + 1)
                        if t == 0:
                            dve.wait_ge(stored, qn * (16 * WINDOWS) + 16)
                        for q in range(2):
                            last = v.scalar_tensor_tensor(
                                out=ob[p:p + WROWS, t // 2].rearrange("p b w -> p (b w)")[:, q::2],
                                in0=ps_w[t][q * WROWS:(q + 1) * WROWS, :], scalar=prm[k][p:p + WROWS, 1:2],
                                in1=x1[g][p:p + WROWS, t // 2].rearrange("p b w -> p (b w)")[:, q::2],
                                op0=ALU.add, op1=ALU.add)
                        last.then_inc(out_ready, 1)

                def steps(m, k, g, last):
                    qn = m * 4 + (2 * k + g)
                    m2, k2, g2 = next_group(m, k, g)
                    down_levels(qn)
                    if not last:
                        make_x1(m2, k2, g2)
                        odd(m2, k2, g2)
                    up_levels(qn)
                    next_trailing(qn)
                    if not last:
                        trailing(qn + 1, g2, range(WINDOWS))
                    finish(qn, k, g)

                dve.wait_ge(const_in, 48)
                v.tensor_copy(down_sb[:], down_raw).then_inc(down_set, 1)
                v.tensor_copy(up_sb[:], up_raw).then_inc(down_set, 1)
                dve.wait_ge(zeroed, N_ZERO)
                dve.sem_inc(out_ready, LEAD)
                make_x1(0, 0, 0)
                odd(0, 0, 0)
                trailing(0, 0, range(WINDOWS))
                pair = groups(steps)
                with dve.Fori(0, C // 2 - 1) as m:
                    pair(m)
                pair(C // 2 - 1, True)


def kernel(**inputs):
    import numpy as np
    import concourse.bacc as bacc
    from concourse.bass_utils import run_bass_kernel_spmd

    a = {k: np.ascontiguousarray(v) for k, v in inputs.items()}
    f = np.float32
    heads = np.repeat(np.arange(NH), HD)
    same = (heads[:, None] == heads[None, :]).astype(f)
    own = (np.arange(NH)[:, None] == heads[None, :]).astype(f)
    head96 = np.concatenate([same, own], 0)
    head8 = np.concatenate([own.T, np.eye(NH, dtype=f)], 0)
    keps = np.concatenate([np.full((C, 1), K_EPS, f), np.zeros((NH, 1), f)], 0)
    per = C // GROUPS
    grp = np.arange(C) // per
    gmean = (grp[:, None] == grp[None, :]).astype(f) / f(per)
    down = np.zeros((128, WINDOWS, HALF), f)
    for t in range(WINDOWS):
        for q in range(2):
            for r in range(HALO, HALO + OROWS):
                row = OROWS * t - HALO + r
                if row < H:
                    down[q * WROWS + r, t, row // 2] = 0.5
    up = np.ascontiguousarray(down.transpose(2, 1, 0))
    inside = np.zeros((128, PAIRW), f)
    for t in range(WINDOWS):
        lo, hi, skip = window_rows(t)
        inside[(t % 2) * WROWS + skip:(t % 2) * WROWS + skip + hi - lo, t // 2] = 1.0

    wqkv = a["L0_conv_w_qkv"]
    feeds = {
        "x": a["x"],
        "wqkv_t": wqkv.T, "wp_t": a["L0_conv_w_proj"].T,
        "gamma": a["L0_conv_gamma"].reshape(C, 1), "beta": a["L0_conv_beta"].reshape(C, 1),
        "base_w": a["L1_conv_base_w"].reshape(C, TAPS * TAPS), "base_b": a["L1_conv_base_b"].reshape(C, 1),
        "base_scale": a["L1_conv_base_scale"].reshape(C, 1),
        "wconv": a["L1_conv_wconv_w"].reshape(3, C, 4, TAPS * TAPS).transpose(1, 0, 2, 3),
        "wscale": a["L1_conv_wscale"].reshape(3, C, 4).transpose(1, 0, 2),
        "ident": np.eye(128, dtype=f), "gmean": gmean, "head96": head96, "head8": head8, "keps": keps,
        "down": down, "up": up, "inside": inside,
    }
    feeds = {k: np.ascontiguousarray(v) for k, v in feeds.items()}
    nc = bacc.Bacc("TRN2", target_bir_lowering=False, num_devices=1)
    args = [nc.dram_tensor(f"in_{k}", v.shape, mybir.dt.from_np(v.dtype), kind="ExternalInput").ap()
            for k, v in feeds.items()]
    out = nc.dram_tensor("out_0", (B, C, H, W), F32, kind="ExternalOutput").ap()
    wt_attention_kernel(nc, *args, out)
    r = run_bass_kernel_spmd(nc, [{f"in_{k}": v for k, v in feeds.items()}], core_ids=[0])
    return r.results[0]["out_0"]
```
